# Optimizing a Trainium2 kernel written in Bass

```python
import numpy as np
import jax
import jax.numpy as jnp

def _softmax(x, axis=-1):
    return jax.nn.softmax(x, axis=axis)

def _gelu(x):
    return jax.nn.gelu(x, approximate=True)

def _silu(x):
    return jax.nn.silu(x)

def _sigmoid(x):
    return jax.nn.sigmoid(x)

def _layernorm(x, axis=-1, eps=1e-05):
    m = jnp.mean(x, axis=axis, keepdims=True)
    v = jnp.var(x, axis=axis, keepdims=True)
    return (x - m) / jnp.sqrt(v + eps)

def _scatter_add(tgt, idx, src, axis=0):
    return tgt.at[idx].add(src)

def _segment_sum(src, seg, n):
    return jax.ops.segment_sum(src, seg, n)
kernel_name = 'mk_cond_seq_d1_seqx_r4_90f3f4'

def setup_inputs(seed: int=0):
    np.random.seed(seed)
    _w = jnp.asarray

    def _rec_inputs():
        import jax
        import jax.numpy as jnp
        _rk = jax.random.key(seed)
        x = -0.0002928 + 1 * jax.random.normal(jax.random.fold_in(_rk, 1), (8, 256, 256), jnp.float32)
        _lenS = 256 - jax.random.randint(jax.random.fold_in(_rk, 7), (8,), 0, max(1, 256 // 4) + 1, jnp.int32)
        _lenS2 = 256 - jax.random.randint(jax.random.fold_in(_rk, 8), (8,), 0, max(1, 256 // 4) + 1, jnp.int32)
        cond_1024 = 0.000887014 + 1.03683 * jax.random.normal(jax.random.fold_in(_rk, 11), (8, 256), jnp.float32)
        _validS = jnp.arange(256)[None, :] < _lenS[:, None]
        _validS2 = jnp.arange(256)[None, :] < _lenS2[:, None]
        _causal = jnp.tril(jnp.ones((256, 256), dtype=bool))
        mask_BxS_bf1 = jnp.ones((8, 256), dtype=bool)
        return (x, cond_1024, mask_BxS_bf1)
    x, cond_1024, mask_BxS_bf1 = _rec_inputs()

    def _L0_cond_setup():
        import jax, jax.numpy as jnp
        import numpy as np
        B, S, H, NH = (2, 512, 256, 16)
        HD = H // NH
        ROT = HD // 2
        COND, FF = (256, 4 * H)
        BASE = 10000.0
        EPS = 1e-05

        def _layer_norm(x, g, b):
            mu = jnp.mean(x, axis=-1, keepdims=True)
            var = jnp.mean(jnp.square(x - mu), axis=-1, keepdims=True)
            return (x - mu) * jax.lax.rsqrt(var + EPS) * g + b

        def _ada_norm(x, cond, g, b, w, bw):
            shift, scale = jnp.split(cond @ w + bw, 2, axis=-1)
            return _layer_norm(x, g, b) * (1.0 + scale[:, None, :]) + shift[:, None, :]

        def _rotary_sin_cos(seq_len):
            inv_freq = 1.0 / BASE ** (jnp.arange(ROT, dtype=jnp.float32) / ROT)
            freqs = jnp.arange(seq_len, dtype=jnp.float32)[:, None] * inv_freq[None, :]
            return (jnp.sin(freqs), jnp.cos(freqs))

        def _apply_rotary(x, sin, cos):
            xe, xo = (x[..., ::2], x[..., 1::2])
            re = xe * cos - xo * sin
            ro = xo * cos + xe * sin
            return jnp.stack((re, ro), axis=-1).reshape(x.shape)

        def _split_heads(x):
            b, s, _ = x.shape
            return x.reshape(b, s, NH, HD).transpose(0, 2, 1, 3)
        key = jax.random.key(seed)
        ks = jax.random.split(key, 16)
        w = lambda k, shape: jax.random.normal(k, shape, dtype=jnp.float32) * 0.02
        z = lambda shape: jnp.zeros(shape, dtype=jnp.float32)
        o = lambda shape: jnp.ones(shape, dtype=jnp.float32)
        return {'x': jax.random.normal(ks[0], (B, S, H), dtype=jnp.float32), 'cond': jax.random.normal(ks[1], (B, COND), dtype=jnp.float32), 'attn_mask': jnp.ones((B, S), dtype=bool), 'wq': w(ks[2], (H, H)), 'bq': z((H,)), 'wk': w(ks[3], (H, H)), 'bk': z((H,)), 'wv': w(ks[4], (H, H)), 'bv': z((H,)), 'wo': w(ks[5], (H, H)), 'bo': z((H,)), 'ln1_g': o((H,)), 'ln1_b': z((H,)), 'ada1_w': w(ks[6], (COND, 2 * H)), 'ada1_b': z((2 * H,)), 'ln2_g': o((H,)), 'ln2_b': z((H,)), 'ada2_w': w(ks[7], (COND, 2 * H)), 'ada2_b': z((2 * H,)), 'ff_w1': w(ks[8], (H, FF)), 'ff_b1': z((FF,)), 'ff_w2': w(ks[9], (FF, H)), 'ff_b2': z((H,))}
    _L0_cond_all = _L0_cond_setup()
    _L0_cond_in = {k: v for k, v in _L0_cond_all.items() if k in ('wq', 'bq', 'wk', 'bk', 'wv', 'bv', 'wo', 'bo', 'ln1_g', 'ln1_b', 'ada1_w', 'ada1_b', 'ln2_g', 'ln2_b', 'ada2_w', 'ada2_b', 'ff_w1', 'ff_b1', 'ff_w2', 'ff_b2')}
    del _L0_cond_all
    return {'x': x, 'cond_1024': cond_1024, 'mask_BxS_bf1': mask_BxS_bf1, 'L0_cond_wq': _L0_cond_in['wq'], 'L0_cond_bq': _L0_cond_in['bq'], 'L0_cond_wk': _L0_cond_in['wk'], 'L0_cond_bk': _L0_cond_in['bk'], 'L0_cond_wv': _L0_cond_in['wv'], 'L0_cond_bv': _L0_cond_in['bv'], 'L0_cond_wo': _L0_cond_in['wo'], 'L0_cond_bo': _L0_cond_in['bo'], 'L0_cond_ln1_g': _L0_cond_in['ln1_g'], 'L0_cond_ln1_b': _L0_cond_in['ln1_b'], 'L0_cond_ada1_w': _L0_cond_in['ada1_w'], 'L0_cond_ada1_b': _L0_cond_in['ada1_b'], 'L0_cond_ln2_g': _L0_cond_in['ln2_g'], 'L0_cond_ln2_b': _L0_cond_in['ln2_b'], 'L0_cond_ada2_w': _L0_cond_in['ada2_w'], 'L0_cond_ada2_b': _L0_cond_in['ada2_b'], 'L0_cond_ff_w1': _L0_cond_in['ff_w1'], 'L0_cond_ff_b1': _L0_cond_in['ff_b1'], 'L0_cond_ff_w2': _L0_cond_in['ff_w2'], 'L0_cond_ff_b2': _L0_cond_in['ff_b2']}

def reference(x, cond_1024, mask_BxS_bf1, L0_cond_wq, L0_cond_bq, L0_cond_wk, L0_cond_bk, L0_cond_wv, L0_cond_bv, L0_cond_wo, L0_cond_bo, L0_cond_ln1_g, L0_cond_ln1_b, L0_cond_ada1_w, L0_cond_ada1_b, L0_cond_ln2_g, L0_cond_ln2_b, L0_cond_ada2_w, L0_cond_ada2_b, L0_cond_ff_w1, L0_cond_ff_b1, L0_cond_ff_w2, L0_cond_ff_b2):
    import jax
    import jax.numpy as jnp

    def _L0_cond_ref(x, cond, attn_mask, wq, bq, wk, bk, wv, bv, wo, bo, ln1_g, ln1_b, ada1_w, ada1_b, ln2_g, ln2_b, ada2_w, ada2_b, ff_w1, ff_b1, ff_w2, ff_b2):
        import jax, jax.numpy as jnp
        import numpy as np
        B, S, H, NH = (2, 512, 256, 16)
        HD = H // NH
        ROT = HD // 2
        COND, FF = (256, 4 * H)
        BASE = 10000.0
        EPS = 1e-05

        def _layer_norm(x, g, b):
            mu = jnp.mean(x, axis=-1, keepdims=True)
            var = jnp.mean(jnp.square(x - mu), axis=-1, keepdims=True)
            return (x - mu) * jax.lax.rsqrt(var + EPS) * g + b

        def _ada_norm(x, cond, g, b, w, bw):
            shift, scale = jnp.split(cond @ w + bw, 2, axis=-1)
            return _layer_norm(x, g, b) * (1.0 + scale[:, None, :]) + shift[:, None, :]

        def _rotary_sin_cos(seq_len):
            inv_freq = 1.0 / BASE ** (jnp.arange(ROT, dtype=jnp.float32) / ROT)
            freqs = jnp.arange(seq_len, dtype=jnp.float32)[:, None] * inv_freq[None, :]
            return (jnp.sin(freqs), jnp.cos(freqs))

        def _apply_rotary(x, sin, cos):
            xe, xo = (x[..., ::2], x[..., 1::2])
            re = xe * cos - xo * sin
            ro = xo * cos + xe * sin
            return jnp.stack((re, ro), axis=-1).reshape(x.shape)

        def _split_heads(x):
            b, s, _ = x.shape
            return x.reshape(b, s, NH, HD).transpose(0, 2, 1, 3)
        residual = x
        h = _ada_norm(x, cond, ln1_g, ln1_b, ada1_w, ada1_b)
        q = _split_heads(h @ wq + bq)
        k = _split_heads(h @ wk + bk)
        v = _split_heads(h @ wv + bv)
        sin, cos = _rotary_sin_cos(x.shape[1])
        q = _apply_rotary(q, sin, cos)
        k = _apply_rotary(k, sin, cos)
        scores = jnp.einsum('bhqd,bhkd->bhqk', q, k) / np.sqrt(HD).astype(np.float32)
        scores = jnp.where(attn_mask[:, None, None, :], scores, -jnp.inf)
        attn = jax.nn.softmax(scores, axis=-1)
        out = jnp.einsum('bhqk,bhkd->bhqd', attn, v)
        out = out.transpose(0, 2, 1, 3).reshape(x.shape[0], x.shape[1], H)
        x = residual + out @ wo + bo
        residual = x
        h = _ada_norm(x, cond, ln2_g, ln2_b, ada2_w, ada2_b)
        ff = jax.nn.gelu(h @ ff_w1 + ff_b1, approximate=False) @ ff_w2 + ff_b2
        return residual + ff
    x = _L0_cond_ref(x, cond_1024, mask_BxS_bf1, L0_cond_wq, L0_cond_bq, L0_cond_wk, L0_cond_bk, L0_cond_wv, L0_cond_bv, L0_cond_wo, L0_cond_bo, L0_cond_ln1_g, L0_cond_ln1_b, L0_cond_ada1_w, L0_cond_ada1_b, L0_cond_ln2_g, L0_cond_ln2_b, L0_cond_ada2_w, L0_cond_ada2_b, L0_cond_ff_w1, L0_cond_ff_b1, L0_cond_ff_w2, L0_cond_ff_b2)
    return x

_drawn_inputs = setup_inputs


def setup_inputs(seed=0):
    import zlib

    import numpy as np

    out = dict(_drawn_inputs(seed))
    spreads = {'L0_cond_bq': (0.0, 0.8),
     'L0_cond_bk': (0.0, 0.8),
     'L0_cond_bv': (0.0, 0.272),
     'L0_cond_bo': (0.0, 0.1),
     'L0_cond_ln1_g': (1.0, 0.6),
     'L0_cond_ln1_b': (0.0, 0.727),
     'L0_cond_ada1_b': (0.0, 0.735),
     'L0_cond_ln2_g': (1.0, 0.6),
     'L0_cond_ln2_b': (0.0, 0.734),
     'L0_cond_ada2_b': (0.0, 0.482),
     'L0_cond_ff_b1': (0.0, 0.1),
     'L0_cond_ff_b2': (0.0, 0.1)}
    factors = {'L0_cond_wq': 8.0, 'L0_cond_wk': 8.0}
    for name, (base, spread) in spreads.items():
        noise = np.random.default_rng([zlib.crc32(name.encode()), seed]).standard_normal(out[name].shape)
        drawn = base * np.exp(spread * noise) if base else spread * noise
        out[name] = jnp.asarray(drawn.astype(out[name].dtype))
    for name, factor in factors.items():
        out[name] = (out[name] * factor).astype(out[name].dtype)
    return out
```

```python
from contextlib import ExitStack

import concourse.bass as bass
from concourse import mybir

ALU = mybir.AluOpType
ACT = mybir.ActivationFunctionType
F32 = mybir.dt.float32
F32R = mybir.dt.float32r
U8 = mybir.dt.uint8
AX_X = mybir.AxisListType.X

P = 128
B, S, H, NH = 8, 256, 256, 16
HD = H // NH
ROT = HD // 2
FF = 4 * H
CC = H // P
TT = S // P
FC = FF // P
EPS = 1e-5
SCALE = float(HD) ** -0.5
MASKED = 1e30
G4 = 4
SLOTS = 2 * NH // G4
HALF = NH // 2

ROW_MASK = 3 * HD
ROWS_A = ROW_MASK + 1
ROW_MAX = ROWS_A
ROWS_B = ROW_MAX + 2

W_QK, W_V = 0, CC * 2 * H
W_O = W_V + CC * H
W_1 = W_O + CC * H
W_2 = W_1 + CC * FF
W_ALL = W_2 + FC * H
W_CHUNK = 1024

VECS = {}
_at = 0
for _name, _n in (("bqk", 4), ("bv", CC), ("ln1_g", CC), ("ln1_b", CC), ("ada1_b", 2 * CC),
                  ("ln2_g", CC), ("ln2_b", CC), ("ada2_b", 2 * CC), ("ff_b1", FC)):
    VECS[_name] = (_at, _n)
    _at += _n
N_VEC = _at

PARTS = ((0, 0), (1, 0), (0, 1))


def block_kernel(nc, x_d, condT_d, mask_row_d, mask_col_d, weights_d, ada_d, vecs_d, rope_d,
                 bo_d, bff2_d, ident_d, out_d):
    ctx = ExitStack()
    with ctx:
        def sb(name, shape, dt=F32):
            return ctx.enter_context(nc.sbuf_tensor(name, shape, dt))

        def ps(name, shape):
            return ctx.enter_context(nc.psum_tensor(name, shape, F32))

        def sem(name):
            return ctx.enter_context(nc.semaphore(name))

        x_sb = sb("x_sb", [P, B * TT, H])
        wts = sb("wts", [P, 2, W_ALL], F32R)
        stage = sb("stage", [P, W_CHUNK])
        vecs = sb("vecs", [P, N_VEC])
        rope = sb("rope", [P, 2, S])
        ident = sb("ident", [P, P])
        bo_bc = sb("bo_bc", [P, H])
        bff2_bc = sb("bff2_bc", [P, H])
        condT = sb("condT", [P, CC, B])
        ada_mod = sb("ada_mod", [P, 2, 2 * CC, B])
        aff = sb("aff", [P, 2, 2, CC, B])
        mask_u8 = sb("mask_u8", [P, B * TT], U8)
        mask_col = sb("mask_col", [P, B * TT])
        mrow_u8 = sb("mrow_u8", [B, S], U8)
        mask_row = sb("mask_row", [B, S], F32R)
        stats = sb("stats", [P, 4, 6])
        mv = sb("mv", [P, 4, 2])
        var_eps = sb("var_eps", [P, 4])
        minus_half = sb("minus_half", [P, 4])
        rstd = sb("rstd", [P, 4])
        rows_n = sb("rows_n", [P, 4, H])
        hs = sb("hs", [P, 2, CC, S], F32R)
        qk32 = sb("qk32", [P, 4, S])
        h32 = qk32[:, 0:CC, :]
        rcos = sb("rcos", [P, 4, S])
        rsin = sb("rsin", [P, 4, S])
        parts = sb("parts", [P, 2, 2, 2, S], F32R)
        qs = sb("qs", [P, 2, NH, S], F32R)
        ks = sb("ks", [P, 2, NH, S], F32R)
        v_all = sb("v_all", [P, B, TT, H])
        v_ones = sb("v_ones", [P, TT, NH, 2 * HD])
        m32 = sb("m32", [P, 2, TT, HALF])
        mparts = sb("mparts", [P, 2, TT, 2, HALF])
        mT = sb("mT", [2 * HALF, 2, S], F32R)
        pT = sb("pT", [P, 2, G4, S])
        oT = sb("oT", [P, NH // G4, S])
        rden = sb("rden", [P, 2 * TT * G4])
        xn = rows_n
        o_n = rows_n[:, TT:2 * TT, :]
        aT32 = sb("aT32", [P, CC, S])
        a_s = sb("a_s", [P, 2, CC, S], F32R)

        ps_max = ps("ps_max", [P, 2, 512])
        ps_sc = ps("ps_sc", [P, 2, G4, S])
        ps_o = ps("ps_o", [P, 512])
        ps_m = ps("ps_m", [P, 512])

        scratch = nc.dram_tensor("scratch", [2, 2, 2, 2, P, S], F32, kind="Internal").ap()
        mask_dram = nc.dram_tensor("mask_dram", [B, S], F32, kind="Internal").ap()

        BT = 4
        NBLK = B * TT // BT
        TB = BT * P
        h2s = qs[:, :, :, :].rearrange("p a h s -> p (a h s)").rearrange(
            "p (t l c n) -> p t l c n", t=NBLK, l=2, c=CC)
        mlp_room = ks[:, :, :, :].rearrange("p a h s -> p (a h s)")
        gs = mlp_room[:, 0:2 * 2 * TB].rearrange("p (f l n) -> p f l n", f=2, l=2)
        h2_32 = rcos[:, :, :].rearrange("p a s -> p (a s)").rearrange("p (c n) -> p c n", c=CC)
        g32 = rsin[:, :, :].rearrange("p a s -> p (a s)").rearrange("p (f n) -> p f n", f=2)
        y_sb = qk32[:, :, :]
        ps_t = ps_max
        ps_f = ps_sc[:, 0, :, :].rearrange("p a s -> p (a s)").rearrange("p (f n) -> p f n", f=2)
        ps_y = ps_sc[:, 1, :, :]

        cond_in, x_in, small_in, ada_in = sem("cond_in"), sem("x_in"), sem("small_in"), sem("ada_in")
        w_in, w_hi, w_split = sem("w_in"), sem("w_hi"), sem("w_split")
        w_first_in, w_first_hi, w_first = sem("w_first_in"), sem("w_first_hi"), sem("w_first")
        stacks_set, v_ones_set, half_set = sem("stacks_set"), sem("v_ones_set"), sem("half_set")
        mask_ready, mask_out, mod_ready, mod_added, aff_half, aff_ready = (
            sem("mask_ready"), sem("mask_out"), sem("mod_ready"), sem("mod_added"), sem("aff_half"), sem("aff_ready"))
        norm_step, xn_ready, xn_turned, h_copied, h_hi, h_lo = (
            sem("norm_step"), sem("xn_ready"), sem("xn_turned"), sem("h_copied"), sem("h_hi"), sem("h_lo"))
        bo_added = sem("bo_added")
        qk_ready, qk_copied, v_ready, v_copied, v_ones_ready = (
            sem("qk_ready"), sem("qk_copied"), sem("v_ready"), sem("v_copied"), sem("v_ones_ready"))
        cos_done, sin_done, even_rotated, odd_rotated, qk_hi, qk_lo = (
            sem("cos_done"), sem("sin_done"), sem("even_rotated"), sem("odd_rotated"), sem("qk_hi"), sem("qk_lo"))
        scratch_written = sem("scratch_written")
        stack_in = [sem("stack_in0"), sem("stack_in1")]
        maxrow_in = [sem("maxrow_in0"), sem("maxrow_in1")]
        max_scores, max_taken, max_hi, max_lo, max_turned, max_copied = (
            sem("max_scores"), sem("max_taken"), sem("max_hi"), sem("max_lo"), sem("max_turned"), sem("max_copied"))
        scores_ready, exp_done, pv_done, o_copied, o_turned = (
            sem("scores_ready"), sem("exp_done"), sem("pv_done"), sem("o_copied"), sem("o_turned"))
        den_done, o_normed, on_turned, a_copied, a_hi, a_lo, attn_ready, attn_added = (
            sem("den_done"), sem("o_normed"), sem("on_turned"), sem("a_copied"), sem("a_hi"), sem("a_lo"),
            sem("attn_ready"), sem("attn_added"))
        var_ready, rstd_ready, n2_step, xn2_ready, xn2_turned, h2_copied, h2_hi, h2_lo, bff2_added = (
            sem("var_ready"), sem("rstd_ready"), sem("n2_step"), sem("xn2_ready"), sem("xn2_turned"), sem("h2_copied"), sem("h2_hi"), sem("h2_lo"),
            sem("bff2_added"))
        f_ready, g_done, g_hi, g_lo, ff2_done, y_added, out_written = (
            sem("f_ready"), sem("g_done"), sem("g_hi"), sem("g_lo"), sem("ff2_done"), sem("y_added"),
            sem("out_written"))

        def wait(eng, s, value):
            if not isinstance(value, int) or value > 0:
                eng.wait_ge(s, value)

        def lead(eng, *counts):
            for count in counts:
                if not isinstance(count, int):
                    eng.compute_val(count)
            eng.wait_ge(stacks_set, 1)

        def has(seq):
            return not isinstance(seq, int) or 0 <= seq < B

        def at(j, *which):
            return isinstance(j, int) and j in which

        def steps(eng, step):
            for j in range(-3, 1):
                step(j, j % 2)
            with eng.Fori(0, (B - 4) // 2) as i:
                step(2 * i + 1, 1)
                step(2 * i + 2, 0)
            for j in range(B - 3, B + 1):
                step(j, j % 2)

        def vec(name, k=0):
            col = VECS[name][0] + k
            return vecs[:, col:col + 1]

        MISC = [
            (0, "max1", 0, max_copied, 2, 2),
            (1, "o1", -1, o_normed, 2, 2),
            (2, "on", -1, a_copied, 1, 1),
            (3, "xn", 3, h_copied, 1, 1),
            (4, "proj_o", -1, attn_added, 1, 1),
            (5, "max0", 1, max_copied, 2, 1),
            (5, "o0", 0, o_normed, 2, 1),
            (5, "qk_even", 3, qk_copied, 2, 1),
            (6, "qk_odd", 3, qk_copied, 2, 2),
            (7, "v", 3, v_copied, 1, 1),
        ]

        def wait_bank(pe, j, index):
            n, jj = index - 1, j
            for _ in range(2 * len(MISC)):
                if n < 0:
                    n, jj = len(MISC) - 1, jj - 1
                _, _, off, s, per, which = MISC[n]
                if has(jj + off):
                    pe.wait_ge(s, (jj + off) * per + which)
                    return
                n -= 1
            pe.wait_ge(mod_added, 2)

        block = ctx.enter_context(nc.Block())

        @block.sync
        def _(sp):
            sp.dma_start(condT[:], condT_d).then_inc(cond_in, 16)
            sp.dma_start(pT[:, :, :, :].rearrange("p a g s -> p (a g s)"), ada_d).then_inc(ada_in, 16)
            for to, frm in ((vecs, vecs_d), (ident, ident_d), (rope, rope_d)):
                sp.dma_start(to[:], frm).then_inc(small_in, 16)
            sp.dma_start(mask_u8[:], mask_col_d).then_inc(small_in, 16)
            sp.dma_start(mrow_u8[:], mask_row_d).then_inc(small_in, 16)
            sp.dma_start(bo_bc[:], bo_d.partition_broadcast(P)).then_inc(small_in, 16)
            sp.dma_start(bff2_bc[:], bff2_d.partition_broadcast(P)).then_inc(small_in, 16)
            for b in range(1, B):
                sp.dma_start(x_sb[:, b * TT:(b + 1) * TT, :],
                             x_d[b].rearrange("(t p) c -> p t c", p=P)).then_inc(x_in, 16)

            sp.wait_ge(mask_ready, 2)
            sp.dma_start(mask_dram, mask_row[:].bitcast(F32)).then_inc(mask_out, 16)

            def load_stack(par, mask, half):
                heads = slice(half * HALF, (half + 1) * HALF)
                for t, k, rows in ((qs, 0, ((0, 0, 2), (2, 0, 1))), (ks, 1, ((0, 0, 1), (1, 0, 2)))):
                    src = scratch[par, k].rearrange("l e (i h) s -> (l e i) h s", h=NH)
                    for to, frm, n in rows:
                        sp.dma_start(t[to * HD:(to + n) * HD, par, heads, :].bitcast(F32),
                                     src[frm * HD:(frm + n) * HD, heads, :]).then_inc(stack_in[half], 16)
                sp.dma_start(ks[ROW_MASK:ROW_MASK + 1, par, heads, :].bitcast(F32),
                             mask.unsqueeze(1).to_broadcast([1, HALF, S])).then_inc(stack_in[half], 16)

            def load_max(par, turned, half):
                lead(sp, turned)
                sp.wait_ge(max_copied, turned)
                for l in range(2):
                    sp.dma_start(qs[ROW_MAX + l:ROW_MAX + l + 1, par, half * HALF:(half + 1) * HALF, :]
                                 .bitcast(F32),
                                 mT[l * HALF:(l + 1) * HALF, half, :].bitcast(F32)
                                 ).then_inc(maxrow_in[half], 16)

            def step(j, par):
                if has(j):
                    load_max(par, 2 * j + 2, 1)
                if has(j + 1):
                    if has(j - 1):
                        lead(sp, SLOTS * j)
                        sp.wait_ge(scores_ready, SLOTS * j)
                    else:
                        sp.wait_ge(stacks_set, 1)
                        sp.wait_ge(mask_out, 16)
                        sp.wait_ge(scratch_written, 16 * (j + 2))
                    load_stack(1 - par, mask_dram[bass.ds(j + 1, 1), :], 1)
                if has(j + 2):
                    lead(sp, j + 3)
                    sp.wait_ge(qk_lo, j + 3)
                    sp.wait_ge(qk_hi, j + 3)
                    if has(j):
                        lead(sp, 80 * (j + 1))
                        sp.wait_ge(stack_in[0], 80 * (j + 1))
                        sp.wait_ge(stack_in[1], 80 * (j + 1))
                    sp.dma_start(scratch[par].rearrange("k l e p s -> p (k l e) s"),
                                 parts[:, :, :, :, :].rearrange("p k l e s -> p (k l e) s").bitcast(F32)
                                 ).then_inc(scratch_written, 16)
                    lead(sp, 16 * (j + 3))
                    sp.wait_ge(scratch_written, 16 * (j + 3))
                    if has(j):
                        lead(sp, SLOTS * j + SLOTS // 2)
                        sp.wait_ge(scores_ready, SLOTS * j + SLOTS // 2)
                    else:
                        sp.wait_ge(stacks_set, 1)
                        sp.wait_ge(mask_out, 16)
                    load_stack(par, mask_dram[bass.ds(j + 2, 1), :], 0)
                if has(j + 1):
                    load_max(1 - par, 2 * j + 3, 0)

            steps(sp, step)
            for t in range(NBLK):
                sp.wait_ge(y_added, t + 1)
                sp.dma_start(out_d[2 * t:2 * t + 2].rearrange("b (t p) c -> p (b t) c", p=P),
                             y_sb).then_inc(out_written, 16)
            sp.wait_ge(out_written, 16 * NBLK)

        @block.gpsimd
        def _(pool):
            pool.memset(qs[0:64, :, :, :].bitcast(F32), 1.0)
            pool.memset(ks[0:64, :, :, :].bitcast(F32), -1.0).then_inc(stacks_set, 1)
            pool.memset(v_ones[:], 0.0).then_inc(v_ones_set, 1)
            pool.memset(minus_half[:], -0.5).then_inc(half_set, 1)

            def split_weights(n):
                cols = slice(n * W_CHUNK, (n + 1) * W_CHUNK)
                pool.wait_ge(w_in, 16 * (n - 1))
                pool.tensor_copy(wts[:, 0, cols], stage[:]).then_inc(w_hi, 1)
                pool.wait_ge(w_hi, n - 1)
                pool.tensor_tensor(wts[:, 1, cols], stage[:], wts[:, 0, cols].bitcast(F32),
                                   ALU.subtract).then_inc(w_split, 1)

            def inverse_deviation(n, count):
                pool.wait_ge(var_ready, count)
                pool.tensor_tensor(rstd[:, 0:n], var_eps[:, 0:n], minus_half[:, 0:n],
                                   ALU.pow).then_inc(rstd_ready, 1)

            def step(j, par):
                if has(j + 3):
                    if at(j, -3):
                        pool.wait_ge(half_set, 1)
                    else:
                        pool.wait_ge(xn_ready, j + 3)
                    inverse_deviation(TT, j + 4)
                    pool.wait_ge(xn_ready, j + 4)
                    if at(j, -3):
                        pool.wait_ge(small_in, 16 * 7)
                    rows = x_sb[:, bass.ds((j + 3) * TT, TT), :]
                    pool.tensor_tensor(rows, rows, bo_bc[:].unsqueeze(1).to_broadcast([P, TT, H]),
                                       ALU.add).then_inc(bo_added, 1)
                    lead(pool)
                    pool.wait_ge(h_copied, j + 4)
                    wait(pool, v_ready, j + 3)
                    pool.tensor_copy(hs[:, 0, :, :], h32).then_inc(h_hi, 1)
                if at(j, -3, -2, -1, 0):
                    split_weights(2 + j + 3)
                if has(j + 1):
                    if at(j, -1):
                        pool.wait_ge(v_ones_set, 1)
                    pool.wait_ge(mask_ready, 2)
                    pool.wait_ge(v_copied, j + 2)
                    wait(pool, pv_done, SLOTS * (j + 1))
                    seq = v_all[:, bass.ds(j + 1, 1), :, :].rearrange("p a t c -> p (a t) c")
                    pool.tensor_copy(v_ones[:, :, :, 0:HD],
                                     seq.rearrange("p t (h d) -> p t h d", d=HD))
                    m = mask_col[:, bass.ds((j + 1) * TT, TT)]
                    pool.tensor_copy(v_ones[:, :, :, HD:HD + 1],
                                     m.unsqueeze(2).unsqueeze(3).to_broadcast([P, TT, NH, 1])
                                     ).then_inc(v_ones_ready, 1)
                if has(j + 3):
                    pool.wait_ge(qk_copied, 2 * (j + 4))
                    wait(pool, even_rotated, j + 3)
                    pool.tensor_tensor(rsin[:], qk32[:],
                                       rope[:, 1:2, :].to_broadcast([P, 4, S]),
                                       ALU.mult).then_inc(sin_done, 1)
                    pool.wait_ge(sin_done, j + 4)
                    pool.wait_ge(cos_done, j + 4)
                    pool.tensor_tensor(rcos[:, 2:4, :], rcos[:, 2:4, :], rsin[:, 0:2, :],
                                       ALU.add).then_inc(odd_rotated, 1)

            steps(pool, step)
            for t in range(NBLK):
                inverse_deviation(BT, B + t + 1)
                pool.wait_ge(xn2_ready, t + 1)
                rows = x_sb[:, t * BT:(t + 1) * BT, :]
                pool.tensor_tensor(rows, rows, bff2_bc[:].unsqueeze(1).to_broadcast([P, BT, H]),
                                   ALU.add).then_inc(bff2_added, 1)

        @block.scalar
        def _(act):
            act.dma_start(x_sb[:, 0:TT, :], x_d[0].rearrange("(t p) c -> p t c", p=P)).then_inc(x_in, 16)
            act.dma_start(stage[:], weights_d[:, 0:W_CHUNK]).then_inc(w_first_in, 16)
            act.dma_start(qk32[:, :, :].rearrange("p a s -> p (a s)"),
                          weights_d[:, W_CHUNK:2 * W_CHUNK]).then_inc(w_first_in, 16)

            def copy_max(seq, half):
                act.wait_ge(max_turned, 2 * seq + half + 1)
                wait(act, maxrow_in[half], 32 * seq)
                act.activation(mT[:, half, :], ps_m[0:2 * HALF, 0:S], ACT.Copy).then_inc(max_copied, 1)

            def load_weights(n):
                if n == 2:
                    act.wait_ge(w_first, 2)
                else:
                    act.wait_ge(w_split, n - 2)
                act.dma_start(stage[:], weights_d[:, n * W_CHUNK:(n + 1) * W_CHUNK]).then_inc(w_in, 16)

            def copy_out(seq, g):
                act.wait_ge(pv_done, SLOTS * seq + 2 * g + 2)
                wait(act, o_turned, 2 * seq - 1 + g // 2)
                act.activation(oT[:, g, :], ps_o[:, 0:S], ACT.Copy).then_inc(o_copied, 1)

            def step(j, par):
                if at(j, -3, -2, -1, 0):
                    load_weights(2 + j + 3)
                for s in range(SLOTS):
                    if has(j):
                        act.wait_ge(scores_ready, SLOTS * j + s + 1)
                        wait(act, pv_done, SLOTS * j + s - 1)
                        act.activation(pT[:, s % 2, :, :], ps_sc[:, s % 2, :, :], ACT.Exp,
                                       scale=SCALE).then_inc(exp_done, 1)
                    if s == 0 and has(j - 1):
                        copy_out(j - 1, 3)
                    if s in (2, 4, 6) and has(j):
                        copy_out(j, s // 2 - 1)
                    if s == 0 and has(j):
                        copy_max(j, 1)
                    if s == 1 and has(j + 2):
                        act.wait_ge(even_rotated, j + 3)
                        act.wait_ge(odd_rotated, j + 3)
                        wait(act, scratch_written, 16 * (j + 2))
                        act.activation(parts[:, :, 0, :, :].rearrange("p k e s -> p e k s"),
                                       rcos[:, :, :].rearrange("p (e k) s -> p e k s", e=2),
                                       ACT.Copy).then_inc(qk_hi, 1)
                    if s == 2 and has(j - 1):
                        act.wait_ge(on_turned, j)
                        wait(act, a_lo, j - 1)
                        for c in range(CC):
                            op = act.activation(aT32[:, c, :], ps_m[:, c * S:(c + 1) * S], ACT.Identity,
                                                bias=vec("bv", c))
                        op.then_inc(a_copied, 1)
                        act.wait_ge(a_copied, j)
                        wait(act, attn_ready, j - 1)
                        act.activation(a_s[:, 0, :, :], aT32[:], ACT.Copy).then_inc(a_hi, 1)
                    if s == 3 and has(j + 3):
                        act.wait_ge(xn_turned, j + 4)
                        if at(j, -3):
                            act.wait_ge(aff_ready, 2)
                            act.wait_ge(w_first, 2)
                        wait(act, cos_done, j + 3)
                        wait(act, sin_done, j + 3)
                        for c in range(CC):
                            op = act.activation(h32[:, c, :], ps_m[:, c * S:(c + 1) * S], ACT.Identity,
                                                scale=aff[:, 0, 0, c, bass.ds(j + 3, 1)],
                                                bias=aff[:, 0, 1, c, bass.ds(j + 3, 1)])
                        op.then_inc(h_copied, 1)
                    if s == 5 and has(j + 1):
                        copy_max(j + 1, 0)
                    if s in (5, 6) and has(j + 3):
                        e = 0 if s == 5 else 1
                        act.wait_ge(qk_ready, 2 * (j + 3) + e + 1)
                        if s == 5:
                            act.wait_ge(h_lo, j + 4)
                        for k in range(2):
                            op = act.activation(qk32[:, 2 * e + k, :], ps_m[:, k * S:(k + 1) * S],
                                                ACT.Identity, bias=vec("bqk", 2 * e + k))
                        op.then_inc(qk_copied, 1)
                    if s == 7 and has(j + 3):
                        act.wait_ge(v_ready, j + 4)
                        if at(j, -3):
                            act.wait_ge(mask_ready, 2)
                        for t in range(TT):
                            op = act.activation(
                                v_all[:, bass.ds(j + 3, 1), t, :].rearrange("p a c -> p (a c)"),
                                ps_m[:, t * H:(t + 1) * H], ACT.Copy,
                                scale=mask_col[:, bass.ds((j + 3) * TT + t, 1)])
                        op.then_inc(v_copied, 1)

            steps(act, step)

            def copy_norm2(t):
                act.wait_ge(xn2_turned, t + 1)
                wait(act, h2_lo, t)
                for c in range(CC):
                    for b in range(2):
                        op = act.activation(h2_32[:, c, b * S:(b + 1) * S],
                                            ps_t[:, c, b * S:(b + 1) * S], ACT.Identity,
                                            scale=aff[:, 1, 0, c, bass.ds(2 * t + b, 1)],
                                            bias=aff[:, 1, 1, c, bass.ds(2 * t + b, 1)])
                op.then_inc(h2_copied, 1)

            copy_norm2(0)
            for t in range(NBLK):
                for f in range(FC):
                    act.wait_ge(f_ready, t * FC + f + 1)
                    wait(act, g_lo, t * FC + f - 1)
                    act.activation(g32[:, f % 2, :], ps_f[:, f % 2, :], ACT.Gelu,
                                   bias=vec("ff_b1", f)).then_inc(g_done, 1)
                    if f == 4 and t + 1 < NBLK:
                        copy_norm2(t + 1)

        @block.vector
        def _(dve):
            dve.wait_ge(small_in, 16 * 7)
            dve.tensor_copy(mask_col[:], mask_u8[:]).then_inc(mask_ready, 1)
            dve.tensor_scalar(mask_row[:], mrow_u8[:], -1.0, MASKED, ALU.add, ALU.mult).then_inc(mask_ready, 1)
            dve.wait_ge(w_first_in, 32)
            first = (stage[:], qk32[:, :, :].rearrange("p a s -> p (a s)"))
            for n in range(2):
                dve.tensor_copy(wts[:, 0, n * W_CHUNK:(n + 1) * W_CHUNK], first[n]).then_inc(w_first_hi, 1)
            for n in range(2):
                cols = slice(n * W_CHUNK, (n + 1) * W_CHUNK)
                dve.wait_ge(w_first_hi, n + 1)
                dve.tensor_tensor(wts[:, 1, cols], first[n], wts[:, 0, cols].bitcast(F32),
                                  ALU.subtract).then_inc(w_first, 1)
            for n in range(2):
                dve.wait_ge(mod_ready, 1)
                first_col = VECS[f"ada{n + 1}_b"][0]
                dve.tensor_tensor(
                    ada_mod[:, n, :, :],
                    ps_m[:, n * 64:n * 64 + 2 * CC * B].rearrange("p (a b) -> p a b", b=B),
                    vecs[:, first_col:first_col + 2 * CC].unsqueeze(2).to_broadcast([P, 2 * CC, B]),
                    ALU.add).then_inc(mod_added, 1)
                dve.wait_ge(mod_added, n + 1)
                for c in range(CC):
                    dve.tensor_scalar(aff[:, n, 0, c, :], ada_mod[:, n, CC + c, :], 1.0,
                                      vec(f"ln{n + 1}_g", c), ALU.add, ALU.mult)
                    dve.tensor_scalar(aff[:, n, 1, c, :], ada_mod[:, n, CC + c, :], 1.0,
                                      vec(f"ln{n + 1}_b", c), ALU.add, ALU.mult).then_inc(aff_half, 1)
                dve.wait_ge(aff_half, CC * (n + 1))
                dve.tensor_tensor(aff[:, n, 1, :, :], aff[:, n, 1, :, :], ada_mod[:, n, 0:CC, :],
                                  ALU.add).then_inc(aff_ready, 1)

            def norm_stats(seq_tile, n, step_sem, count, rstd_before):
                for t in range(n):
                    op = dve.bn_stats(stats[:, t, :], x_sb[:, bass.ds(seq_tile + t, 1), :].rearrange(
                        "p a c -> p (a c)"))
                op.then_inc(step_sem, 1)
                lead(dve)
                dve.wait_ge(step_sem, count + 1)
                for t in range(n):
                    op = dve.bn_aggr(mv[:, t, :], stats[:, t, :])
                op.then_inc(step_sem, 1)
                dve.wait_ge(step_sem, count + 2)
                wait(dve, rstd_ready, rstd_before)
                dve.tensor_scalar(var_eps[:, 0:n], mv[:, 0:n, 1:2].rearrange("p n a -> p (n a)"),
                                  EPS, None, ALU.add).then_inc(var_ready, 1)

            def norm_rows(seq_tile, n, rstd_count, ready):
                dve.wait_ge(rstd_ready, rstd_count)
                for t in range(n):
                    op = dve.tensor_scalar(xn[:, t, :], x_sb[:, bass.ds(seq_tile + t, 1), :].rearrange(
                        "p a c -> p (a c)"), mv[:, t, 0:1], rstd[:, t:t + 1], ALU.subtract, ALU.mult)
                op.then_inc(ready, 1)

            def split_max(seq, half):
                dve.wait_ge(max_taken, NH * seq + HALF * (half + 1))
                wait(dve, max_turned, 2 * (seq - 1) + half + 1)
                dve.tensor_copy(mparts[:, half, :, 0, :].bitcast(F32R), m32[:, half, :, :]).then_inc(max_hi, 1)
                dve.wait_ge(max_hi, 2 * seq + half + 1)
                dve.tensor_tensor(mparts[:, half, :, 1, :], m32[:, half, :, :], mparts[:, half, :, 0, :],
                                  ALU.subtract).then_inc(max_lo, 1)

            def normalise(seq, pair):
                dve.wait_ge(o_turned, 2 * seq + pair + 1)
                dve.reciprocal(rden[:], ps_m[:, :].rearrange("p (n d) -> p n d", d=2 * HD)[:, :, HD:HD + 1]
                               .rearrange("p n a -> p (n a)")).then_inc(den_done, 1)
                dve.wait_ge(den_done, 2 * seq + pair + 1)
                wait(dve, on_turned, seq)
                num = ps_m[:, :].rearrange("p (g t j d) -> p g t j d", g=2, t=TT, j=G4)
                den = rden[:].rearrange("p (g t j) -> p g t j", g=2, t=TT)
                for t in range(TT):
                    op = dve.tensor_tensor(
                        o_n[:, t, pair * P:(pair + 1) * P].rearrange("p (g j d) -> p g j d", g=2, j=G4),
                        num[:, :, t, :, 0:HD],
                        den[:, :, t, :].unsqueeze(3).to_broadcast([P, 2, G4, HD]), ALU.mult)
                op.then_inc(o_normed, 1)

            def step(j, par):
                for s in range(SLOTS):
                    if has(j + 1):
                        for h in (2 * s, 2 * s + 1):
                            dve.wait_ge(max_scores, NH * (j + 1) + h + 1)
                            if h % HALF == 0:
                                wait(dve, max_lo, 2 * j + h // HALF + 1)
                            dve.tensor_reduce(
                                m32[:, h // HALF, :, h % HALF:h % HALF + 1].rearrange("p t a -> p (t a)"),
                                ps_max[:, h % 2, :].rearrange("p (t n) -> p t n", t=TT),
                                AX_X, ALU.max).then_inc(max_taken, 1)
                    if s == 0 and has(j + 2):
                        dve.wait_ge(sin_done, j + 3)
                        dve.wait_ge(cos_done, j + 3)
                        dve.tensor_tensor(rcos[:, 0:2, :], rcos[:, 0:2, :], rsin[:, 2:4, :],
                                          ALU.subtract).then_inc(even_rotated, 1)
                    if s == 0 and has(j + 3):
                        if isinstance(j, int) and j + 3 < 1:
                            dve.wait_ge(x_in, 16 * B)
                        norm_stats((j + 3) * TT, TT, norm_step, 2 * (j + 3), j + 3)
                    if s == 1 and has(j - 1):
                        normalise(j - 1, 1)
                    if s == 1 and has(j + 2):
                        dve.wait_ge(qk_hi, j + 3)
                        dve.wait_ge(even_rotated, j + 3)
                        dve.wait_ge(odd_rotated, j + 3)
                        for e in range(2):
                            op = dve.tensor_tensor(parts[:, :, 1, e, :], rcos[:, 2 * e:2 * e + 2, :],
                                                   parts[:, :, 0, e, :].bitcast(F32), ALU.subtract)
                        op.then_inc(qk_lo, 1)
                    if s == 2 and has(j + 3):
                        wait(dve, xn_turned, j + 3)
                        norm_rows((j + 3) * TT, TT, j + 4, xn_ready)
                    if s == 4 and has(j + 3):
                        dve.wait_ge(h_hi, j + 4)
                        dve.tensor_tensor(hs[:, 1, :, :], h32, hs[:, 0, :, :].bitcast(F32),
                                          ALU.subtract).then_inc(h_lo, 1)
                    if s == 3 and has(j - 1):
                        dve.wait_ge(a_hi, j)
                        dve.tensor_tensor(a_s[:, 1, :, :], aT32[:], a_s[:, 0, :, :].bitcast(F32),
                                          ALU.subtract).then_inc(a_lo, 1)
                    if s == 3 and has(j + 1):
                        split_max(j + 1, 0)
                    if s == 4 and has(j - 1):
                        dve.wait_ge(attn_ready, j)
                        dve.wait_ge(bo_added, j)
                        rows = x_sb[:, bass.ds((j - 1) * TT, TT), :]
                        dve.tensor_tensor(rows, ps_m[:, :].rearrange("p (t c) -> p t c", t=TT), rows,
                                          ALU.add).then_inc(attn_added, 1)
                    if s == 5 and has(j):
                        normalise(j, 0)
                    if s == 7 and has(j + 3):
                        dve.wait_ge(qk_copied, 2 * (j + 4))
                        wait(dve, qk_lo, j + 3)
                        dve.tensor_tensor(rcos[:], qk32[:], rope[:, 0:1, :].to_broadcast([P, 4, S]),
                                          ALU.mult).then_inc(cos_done, 1)
                    if s == 7 and has(j + 1):
                        split_max(j + 1, 1)

            steps(dve, step)

            def norm2(t):
                if t == 0:
                    dve.wait_ge(attn_added, B)
                    dve.wait_ge(xn_turned, B)
                else:
                    dve.wait_ge(xn2_turned, t)
                norm_stats(t * BT, BT, n2_step, 2 * t, B + t)
                norm_rows(t * BT, BT, B + t + 1, xn2_ready)

            def split_norm2(t):
                dve.wait_ge(h2_copied, t + 1)
                dve.tensor_copy(h2s[:, t, 0, :, :], h2_32).then_inc(h2_hi, 1)
                dve.wait_ge(h2_hi, t + 1)
                dve.tensor_tensor(h2s[:, t, 1, :, :], h2_32, h2s[:, t, 0, :, :].bitcast(F32),
                                  ALU.subtract).then_inc(h2_lo, 1)

            norm2(0)
            split_norm2(0)
            for t in range(NBLK):
                for f in range(FC):
                    dve.wait_ge(g_done, t * FC + f + 1)
                    wait(dve, ff2_done, t * FC + f - 1)
                    dve.tensor_copy(gs[:, f % 2, 0, :], g32[:, f % 2, :]).then_inc(g_hi, 1)
                    dve.wait_ge(g_hi, t * FC + f + 1)
                    dve.tensor_tensor(gs[:, f % 2, 1, :], g32[:, f % 2, :], gs[:, f % 2, 0, :].bitcast(F32),
                                      ALU.subtract).then_inc(g_lo, 1)
                    if f == 0 and t + 1 < NBLK:
                        norm2(t + 1)
                    if f == 5 and t + 1 < NBLK:
                        split_norm2(t + 1)
                dve.wait_ge(ff2_done, (t + 1) * FC)
                dve.wait_ge(bff2_added, t + 1)
                wait(dve, out_written, 16 * t)
                dve.tensor_tensor(y_sb, ps_y, x_sb[:, t * BT:(t + 1) * BT, :], ALU.add).then_inc(y_added, 1)

        @block.tensor
        def _(pe):
            pe.wait_ge(cond_in, 16)
            pe.wait_ge(ada_in, 16)
            ada = pT[:, :, :, :].rearrange("p a g s -> p (a g s)").rearrange(
                "p (n c m) -> p n c m", n=2, c=CC)
            for n in range(2):
                for m in range(2 * CC):
                    for c in range(CC):
                        op = pe.matmul(ps_m[:, n * 64 + m * B:n * 64 + (m + 1) * B],
                                       ada[:, n, c, m * P:(m + 1) * P], condT[:, c, :],
                                       start=(c == 0), stop=(c == CC - 1))
            op.then_inc(mod_ready, 1)
            pe.wait_ge(small_in, 16 * 7)

            def w(l, col, n):
                return wts[:, l, col:col + n]

            def score_max(seq, par, h):
                if h % HALF == 0:
                    pe.wait_ge(stack_in[h // HALF], 80 * (seq + 1))
                wait(pe, max_taken, NH * seq + h - 1)
                for t in range(TT):
                    op = pe.matmul(ps_max[:, h % 2, t * S:(t + 1) * S],
                                   qs[0:ROWS_A, par, h, t * P:(t + 1) * P], ks[0:ROWS_A, par, h, :],
                                   start=True, stop=True)
                op.then_inc(max_scores, 1)

            def score_exp(seq, par, s):
                g, kt = s // 2, s % 2
                if s % (SLOTS // 2) == 0:
                    pe.wait_ge(maxrow_in[s // (SLOTS // 2)], 32 * (seq + 1))
                wait(pe, exp_done, SLOTS * seq + s - 1)
                for i in range(G4):
                    h = g * G4 + i
                    op = pe.matmul(ps_sc[:, s % 2, i, :], ks[0:ROWS_B, par, h, kt * P:(kt + 1) * P],
                                   qs[0:ROWS_B, par, h, :], start=True, stop=True)
                op.then_inc(scores_ready, 1)

            def times_v(seq, s):
                g, kt = s // 2, s % 2
                if s == 0:
                    pe.wait_ge(v_ones_ready, seq + 1)
                pe.wait_ge(exp_done, SLOTS * seq + s + 1)
                if kt == 0:
                    wait(pe, o_copied, NH // G4 * seq + g)
                for i in range(G4):
                    op = pe.matmul(ps_o[i * 32:(i + 1) * 32, 0:S], v_ones[:, kt, g * G4 + i, :],
                                   pT[:, s % 2, i, :], start=(kt == 0), stop=(kt == TT - 1))
                op.then_inc(pv_done, 1)

            def turn_max(seq, half):
                pe.wait_ge(max_lo, 2 * seq + half + 1)
                for t in range(TT):
                    op = pe.transpose(ps_m[0:2 * HALF, t * P:(t + 1) * P],
                                      mparts[:, half, t, :, :].rearrange("p l h -> p (l h)"), ident[:])
                op.then_inc(max_turned, 1)

            def turn_out(seq, pair):
                pe.wait_ge(o_copied, NH // G4 * seq + 2 * pair + 2)
                for g in range(2):
                    for t in range(TT):
                        col = (g * TT + t) * P
                        op = pe.transpose(ps_m[:, col:col + P], oT[:, 2 * pair + g, t * P:(t + 1) * P], ident[:])
                op.then_inc(o_turned, 1)

            def turn_rows(src, done):
                for c in range(CC):
                    for t in range(TT):
                        op = pe.transpose(ps_m[:, c * S + t * P:c * S + (t + 1) * P],
                                          src[:, t, c * P:(c + 1) * P], ident[:])
                op.then_inc(done, 1)

            def rows_times(acts, col, done):
                for t in range(TT):
                    for n, (lw, la) in enumerate(PARTS):
                        for c in range(CC):
                            op = pe.matmul(ps_m[:, t * H:(t + 1) * H], acts[:, la, c, t * P:(t + 1) * P],
                                           w(lw, col + c * H, H), start=(n == 0 and c == 0),
                                           stop=(n == 2 and c == CC - 1))
                op.then_inc(done, 1)

            def misc(j, name):
                if name == "max1":
                    turn_max(j, 1)
                if name == "max0":
                    turn_max(j + 1, 0)
                if name == "o1":
                    turn_out(j - 1, 1)
                if name == "o0":
                    turn_out(j, 0)
                if name == "on":
                    pe.wait_ge(o_normed, 2 * j)
                    turn_rows(o_n, on_turned)
                if name == "xn":
                    pe.wait_ge(xn_ready, j + 4)
                    turn_rows(xn, xn_turned)
                if name == "proj_o":
                    pe.wait_ge(a_lo, j)
                    rows_times(a_s, W_O, attn_ready)
                if name == "v":
                    rows_times(hs, W_V, v_ready)
                if name in ("qk_even", "qk_odd"):
                    e = 0 if name == "qk_even" else 1
                    if e == 0:
                        pe.wait_ge(h_lo, j + 4)
                        if at(j, -3):
                            pe.wait_ge(w_first, 2)
                    for k in range(2):
                        for n, (lw, la) in enumerate(PARTS):
                            for c in range(CC):
                                op = pe.matmul(ps_m[:, k * S:(k + 1) * S],
                                               w(lw, W_QK + (c * 4 + 2 * e + k) * P, P), hs[:, la, c, :],
                                               start=(n == 0 and c == 0), stop=(n == 2 and c == CC - 1))
                    op.then_inc(qk_ready, 1)

            def step(j, par):
                for s in range(SLOTS):
                    if has(j):
                        score_exp(j, par, s)
                    if has(j + 1):
                        score_max(j + 1, 1 - par, 2 * s)
                        score_max(j + 1, 1 - par, 2 * s + 1)
                    if s == 0 and has(j - 1):
                        times_v(j - 1, SLOTS - 1)
                    if s > 0 and has(j):
                        times_v(j, s - 1)
                    for index, (slot, name, off, _, _, _) in enumerate(MISC):
                        if slot == s and has(j + off):
                            wait_bank(pe, j, index)
                            misc(j, name)

            steps(pe, step)

            def turn_norm2(t):
                pe.wait_ge(xn2_ready, t + 1)
                wait(pe, h2_copied, t)
                for c in range(CC):
                    for i in range(BT):
                        op = pe.transpose(ps_t[:, c, i * P:(i + 1) * P], xn[:, i, c * P:(c + 1) * P], ident[:])
                op.then_inc(xn2_turned, 1)

            def ff1(t, f):
                if f == 0:
                    pe.wait_ge(h2_lo, t + 1)
                wait(pe, g_done, t * FC + f - 1)
                for n, (lw, la) in enumerate(PARTS):
                    for c in range(CC):
                        op = pe.matmul(ps_f[:, f % 2, :], w(lw, W_1 + c * FF + f * P, P), h2s[:, t, la, c, :],
                                       start=(n == 0 and c == 0), stop=(n == 2 and c == CC - 1))
                op.then_inc(f_ready, 1)

            def ff2(t, f):
                pe.wait_ge(g_lo, t * FC + f + 1)
                if f == 0:
                    wait(pe, y_added, t)
                for i in range(BT):
                    for n, (lw, la) in enumerate(PARTS):
                        op = pe.matmul(ps_y[:, i, :], gs[:, f % 2, la, i * P:(i + 1) * P],
                                       w(lw, W_2 + f * H, H), start=(f == 0 and n == 0 and i % 2 == 0),
                                       stop=(f == FC - 1 and n == 2), skip_group_check=True)
                op.then_inc(ff2_done, 1)

            pe.wait_ge(w_split, 4)
            turn_norm2(0)
            for t in range(NBLK):
                ff1(t, 0)
                ff1(t, 1)
                for f in range(FC):
                    ff2(t, f)
                    if f + 2 < FC:
                        ff1(t, f + 2)
                    if f == 2 and t + 1 < NBLK:
                        turn_norm2(t + 1)


def _chunks(a):
    c = a.shape[0] // P
    return a.reshape(c, P, -1).transpose(1, 0, 2).reshape(P, -1)


def kernel(**inputs):
    import numpy as np
    import concourse.bacc as bacc
    from concourse.bass_utils import run_bass_kernel_spmd

    a = {k.removeprefix("L0_cond_"): np.asarray(v) for k, v in inputs.items()}

    def rotary_columns(w, odd):
        return w.reshape(w.shape[0], NH, ROT, 2)[:, :, :, odd].transpose(0, 2, 1).reshape(w.shape[0], P)

    qk = np.concatenate([rotary_columns(a[n], odd) for odd in (0, 1) for n in ("wq", "wk")], axis=1)
    weights = np.concatenate([_chunks(w) for w in (qk, a["wv"], a["wo"], a["ff_w1"], a["ff_w2"])], axis=1)
    bqk = np.concatenate([rotary_columns(a[n][None], odd) for odd in (0, 1) for n in ("bq", "bk")], axis=0)
    vecs = np.concatenate([bqk.T] + [a[n].reshape(-1, P).T for n in (
        "bv", "ln1_g", "ln1_b", "ada1_b", "ln2_g", "ln2_b", "ada2_b", "ff_b1")], axis=1)
    inv = (np.float32(1.0) / np.power(np.float32(10000.0), np.arange(ROT, dtype=np.float32) / np.float32(ROT)))
    ang = np.arange(S, dtype=np.float32)[:, None] * inv.astype(np.float32)[None, :]
    rope = np.stack([np.cos(ang), np.sin(ang)]).transpose(2, 0, 1).astype(np.float32)
    arrays = {
        "x": a["x"],
        "condT": a["cond_1024"].reshape(B, CC, P).transpose(2, 1, 0),
        "mask_row": a["mask_BxS_bf1"].view(np.uint8),
        "mask_col": a["mask_BxS_bf1"].view(np.uint8).reshape(B * TT, P).T,
        "weights": weights,
        "ada": np.concatenate([_chunks(a["ada1_w"]), _chunks(a["ada2_w"])], axis=1),
        "vecs": vecs,
        "rope": np.repeat(rope, NH, axis=0),
        "bo": a["bo"],
        "bff2": a["ff_b2"],
        "ident": np.eye(P, dtype=np.float32),
    }
    arrays = {f"{k}_dram": np.ascontiguousarray(v) for k, v in arrays.items()}
    nc = bacc.Bacc("TRN2", target_bir_lowering=False, num_devices=1)
    args = [nc.dram_tensor(k, v.shape, mybir.dt.from_np(v.dtype), kind="ExternalInput").ap()
            for k, v in arrays.items()]
    out = nc.dram_tensor("out_dram", (B, S, H), F32, kind="ExternalOutput").ap()
    block_kernel(nc, *args, out)
    r = run_bass_kernel_spmd(nc, [arrays], core_ids=[0])
    return r.results[0]["out_dram"]
```

```python
from contextlib import ExitStack

import concourse.bass as bass
from concourse import mybir

ALU = mybir.AluOpType
ACT = mybir.ActivationFunctionType
F32 = mybir.dt.float32
F32R = mybir.dt.float32r
U8 = mybir.dt.uint8
AX_X = mybir.AxisListType.X

P = 128
B, S, H, NH = 8, 256, 256, 16
HD = H // NH
ROT = HD // 2
FF = 4 * H
CC = H // P
TT = S // P
FC = FF // P
EPS = 1e-5
SCALE = float(HD) ** -0.5
MASKED = 1e30
G4 = 4
CHUNKS = 2 * NH // 2
SLOTS = 2 * NH // G4
HALF = NH // 2

ROW_MASK = 3 * HD
ROWS_A = ROW_MASK + 1
ROW_MAX = ROWS_A
ROWS_B = ROW_MAX + 2

W_QK, W_V = 0, CC * 2 * H
W_O = W_V + CC * H
W_1 = W_O + CC * H
W_2 = W_1 + CC * FF
W_ALL = W_2 + FC * H
W_CHUNK = 1024

VECS = {}
_at = 0
for _name, _n in (("bqk", 4), ("bv", CC), ("ln1_g", CC), ("ln1_b", CC), ("ada1_b", 2 * CC),
                  ("ln2_g", CC), ("ln2_b", CC), ("ada2_b", 2 * CC), ("ff_b1", FC)):
    VECS[_name] = (_at, _n)
    _at += _n
N_VEC = _at

PARTS = ((0, 0), (1, 0), (0, 1))


def block_kernel(nc, x_d, condT_d, mask_row_d, mask_col_d, weights_d, ada_d, vecs_d, rope_d,
                 bo_d, bff2_d, ident_d, out_d):
    ctx = ExitStack()
    with ctx:
        def sb(name, shape, dt=F32):
            return ctx.enter_context(nc.sbuf_tensor(name, shape, dt))

        def ps(name, shape):
            return ctx.enter_context(nc.psum_tensor(name, shape, F32))

        def sem(name):
            return ctx.enter_context(nc.semaphore(name))

        x_sb = sb("x_sb", [P, B * TT, H])
        wts = sb("wts", [P, 2, W_ALL], F32R)
        stage = sb("stage", [P, W_CHUNK])
        vecs = sb("vecs", [P, N_VEC])
        rope = sb("rope", [P, 2, S])
        ident = sb("ident", [P, P])
        bo_bc = sb("bo_bc", [P, H])
        bff2_bc = sb("bff2_bc", [P, H])
        condT = sb("condT", [P, CC, B])
        ada_mod = sb("ada_mod", [P, 2, 2 * CC, B])
        aff = sb("aff", [P, 2, 2, CC, B])
        mask_u8 = sb("mask_u8", [P, B * TT], U8)
        mask_col = sb("mask_col", [P, B * TT])
        mrow_u8 = sb("mrow_u8", [B, S], U8)
        mask_row = sb("mask_row", [B, S], F32R)
        stats = sb("stats", [P, 4, 6])
        mv = sb("mv", [P, 4, 2])
        var_eps = sb("var_eps", [P, 4])
        minus_half = sb("minus_half", [P, 4])
        rstd = sb("rstd", [P, 4])
        rows_n = sb("rows_n", [P, 4, H])
        hs = sb("hs", [P, 2, CC, S], F32R)
        qk32 = sb("qk32", [P, 4, S])
        h32 = qk32[:, 0:CC, :]
        rcos = sb("rcos", [P, 4, S])
        rsin = sb("rsin", [P, 4, S])
        parts = sb("parts", [P, 2, 2, 2, S], F32R)
        qs = sb("qs", [P, 2, NH, S], F32R)
        ks = sb("ks", [P, 2, NH, S], F32R)
        v_all = sb("v_all", [P, 4, TT, H])
        v_ones = sb("v_ones", [P, 2, TT, NH, 2 * HD])
        m32 = sb("m32", [P, 2, TT, HALF])
        mparts = sb("mparts", [P, 2, TT, 2, HALF])
        mT = sb("mT", [2 * HALF, 2, S], F32R)
        pT = sb("pT", [P, 2, G4, S])
        oT = sb("oT", [P, NH // G4, S])
        rden = sb("rden", [P, 2 * TT * G4])
        xn = rows_n
        o_n = rows_n[:, TT:2 * TT, :]
        aT32 = sb("aT32", [P, CC, S])
        a_s = sb("a_s", [P, 2, CC, S], F32R)

        ps_max = ps("ps_max", [P, 2, 512])
        ps_sc = ps("ps_sc", [P, 3, 2, S])
        ps_o = ps("ps_o", [P, 512])
        ps_m2 = ps("ps_m", [P, 2, 512])
        ps_m = ps_m2[:, 0, :]

        scratch = nc.dram_tensor("scratch", [2, 2, 2, 2, P, S], F32, kind="Internal").ap()
        mask_dram = nc.dram_tensor("mask_dram", [B, S], F32, kind="Internal").ap()

        BT = 4
        NBLK = B * TT // BT
        TB = BT * P
        h2s = qs[:, :, :, :].rearrange("p a h s -> p (a h s)").rearrange(
            "p (t l c n) -> p t l c n", t=NBLK, l=2, c=CC)
        mlp_room = ks[:, :, :, :].rearrange("p a h s -> p (a h s)")
        AHEAD = 4
        FF1_AHEAD = {1: 0, 3: 1, 4: 2, 5: 3}
        GELU_AHEAD = {2: 0, 3: 1, 5: 2}
        LO_AHEAD = {3: 0, 5: 1}
        gs = mlp_room[:, 0:AHEAD * 2 * TB].rearrange("p (f l n) -> p f l n", f=AHEAD, l=2)
        h2_32 = rcos[:, :, :].rearrange("p a s -> p (a s)").rearrange("p (c n) -> p c n", c=CC)
        g32 = rsin[:, :, :].rearrange("p a s -> p (a s)").rearrange("p (f n) -> p f n", f=2)
        y_sb = qk32[:, :, :]
        ps_t = ps_max
        ps_f = ps_sc[:, :, :, :].rearrange("p f a s -> p f (a s)")
        xn2 = v_all[:, 0:BT // TT, :, :].rearrange("p a t c -> p (a t) c")
        ps_y = ps_m2[:, :, :].rearrange("p a (i c) -> p (a i) c", i=2)

        cond_in, x_in, small_in, ada_in = sem("cond_in"), sem("x_in"), sem("small_in"), sem("ada_in")
        w_in, w_hi, w_split = sem("w_in"), sem("w_hi"), sem("w_split")
        w_first_in, w_first_hi, w_first = sem("w_first_in"), sem("w_first_hi"), sem("w_first")
        stacks_set, v_ones_set, half_set = sem("stacks_set"), sem("v_ones_set"), sem("half_set")
        mask_ready, mask_out, mod_ready, mod_added, aff_half, aff_ready = (
            sem("mask_ready"), sem("mask_out"), sem("mod_ready"), sem("mod_added"), sem("aff_half"), sem("aff_ready"))
        norm_step, xn_ready, xn_turned, h_copied, h_hi, h_lo = (
            sem("norm_step"), sem("xn_ready"), sem("xn_turned"), sem("h_copied"), sem("h_hi"), sem("h_lo"))
        bo_added = sem("bo_added")
        qk_ready, qk_copied, v_ready, v_copied, v_ones_ready = (
            sem("qk_ready"), sem("qk_copied"), sem("v_ready"), sem("v_copied"), sem("v_ones_ready"))
        cos_done, sin_done, even_rotated, odd_rotated, qk_hi, qk_lo = (
            sem("cos_done"), sem("sin_done"), sem("even_rotated"), sem("odd_rotated"), sem("qk_hi"), sem("qk_lo"))
        hi_written, lo_written = sem("hi_written"), sem("lo_written")
        stack_in = [sem("stack_in0"), sem("stack_in1")]
        maxrow_in = [sem("maxrow_in0"), sem("maxrow_in1")]
        max_scores, max_taken, max_hi, max_lo, max_turned, max_copied = (
            sem("max_scores"), sem("max_taken"), sem("max_hi"), sem("max_lo"), sem("max_turned"), sem("max_copied"))
        scores_ready, exp_done, pv_done, o_copied, o_turned = (
            sem("scores_ready"), sem("exp_done"), sem("pv_done"), sem("o_copied"), sem("o_turned"))
        den_done, o_normed, on_turned, a_copied, a_hi, a_lo, attn_ready, attn_added = (
            sem("den_done"), sem("o_normed"), sem("on_turned"), sem("a_copied"), sem("a_hi"), sem("a_lo"),
            sem("attn_ready"), sem("attn_added"))
        var_ready, rstd_ready, n2_step, xn2_ready, xn2_turned, h2_copied, h2_hi, h2_lo, bff2_added = (
            sem("var_ready"), sem("rstd_ready"), sem("n2_step"), sem("xn2_ready"), sem("xn2_turned"), sem("h2_copied"), sem("h2_hi"), sem("h2_lo"),
            sem("bff2_added"))
        f_ready, g_done, g_hi, g_lo, ff2_done, y_ready, y_added, out_written = (
            sem("f_ready"), sem("g_done"), sem("g_hi"), sem("g_lo"), sem("ff2_done"), sem("y_ready"), sem("y_added"),
            [sem("out_written0"), sem("out_written1")])

        def wait(eng, s, value):
            if not isinstance(value, int) or value > 0:
                eng.wait_ge(s, value)

        def lead(eng, *counts):
            for count in counts:
                if not isinstance(count, int):
                    eng.compute_val(count)
            eng.wait_ge(stacks_set, 1)

        def has(seq):
            return not isinstance(seq, int) or 0 <= seq < B

        def at(j, *which):
            return isinstance(j, int) and j in which

        def steps(eng, step):
            for j in range(-3, 1):
                step(j, j % 2)
            with eng.Fori(0, (B - 4) // 2) as i:
                step(2 * i + 1, 1)
                step(2 * i + 2, 0)
            for j in range(B - 3, B + 1):
                step(j, j % 2)

        def vec(name, k=0):
            col = VECS[name][0] + k
            return vecs[:, col:col + 1]

        EARLY = 100
        MISC = [
            (0, "v", 2, v_copied, 1, 1),
            (1, "max1", 0, max_copied, 2, 2),
            (EARLY + 2, "o1", -1, o_normed, 2, 2),
            (2, "xn", 3, h_copied, 1, 1),
            (3, "on", -1, a_copied, 1, 1),
            (4, "max0", 1, max_copied, 2, 1),
            (5, "qk_even", 3, qk_copied, 2, 1),
            (5, "o0", 0, o_normed, 2, 1),
            (6, "qk_odd", 3, qk_copied, 2, 2),
            (EARLY + 7, "proj_o", -1, attn_added, 1, 1),
        ]
        BANK = {name: n % 2 for n, (_, name, *_) in enumerate(MISC)}

        def wait_bank(pe, j, index):
            n, jj = index - 2, j
            for _ in range(2 * len(MISC)):
                if n < 0:
                    n, jj = n + len(MISC), jj - 1
                _, _, off, s, per, which = MISC[n]
                if has(jj + off):
                    pe.wait_ge(s, (jj + off) * per + which)
                    return
                n -= 2
            pe.wait_ge(mod_added, 2)

        block = ctx.enter_context(nc.Block())

        @block.sync
        def _(sp):
            sp.dma_start(condT[:], condT_d).then_inc(cond_in, 16)
            sp.dma_start(pT[:, :, :, :].rearrange("p a g s -> p (a g s)"), ada_d).then_inc(ada_in, 16)
            for to, frm in ((vecs, vecs_d), (ident, ident_d), (rope, rope_d)):
                sp.dma_start(to[:], frm).then_inc(small_in, 16)
            sp.dma_start(mask_u8[:], mask_col_d).then_inc(small_in, 16)
            sp.dma_start(mrow_u8[:], mask_row_d).then_inc(small_in, 16)
            sp.dma_start(bo_bc[:], bo_d.partition_broadcast(P)).then_inc(small_in, 16)
            sp.dma_start(bff2_bc[:], bff2_d.partition_broadcast(P)).then_inc(small_in, 16)
            for b in range(1, B):
                sp.dma_start(x_sb[:, b * TT:(b + 1) * TT, :],
                             x_d[b].rearrange("(t p) c -> p t c", p=P)).then_inc(x_in, 16)

            sp.wait_ge(mask_ready, 2)
            sp.dma_start(mask_dram, mask_row[:].bitcast(F32)).then_inc(mask_out, 16)

            def load_stack(par, mask, half):
                heads = slice(half * HALF, (half + 1) * HALF)
                for t, k, rows in ((qs, 0, ((0, 0, 2), (2, 0, 1))), (ks, 1, ((0, 0, 1), (1, 0, 2)))):
                    src = scratch[par, k].rearrange("l e (i h) s -> (l e i) h s", h=NH)
                    for to, frm, n in rows:
                        sp.dma_start(t[to * HD:(to + n) * HD, par, heads, :].bitcast(F32),
                                     src[frm * HD:(frm + n) * HD, heads, :]).then_inc(stack_in[half], 16)
                sp.dma_start(ks[ROW_MASK:ROW_MASK + 1, par, heads, :].bitcast(F32),
                             mask.unsqueeze(1).to_broadcast([1, HALF, S])).then_inc(stack_in[half], 16)

            def load_max(par, turned, half):
                lead(sp, turned)
                sp.wait_ge(max_copied, turned)
                for l in range(2):
                    sp.dma_start(qs[ROW_MAX + l:ROW_MAX + l + 1, par, half * HALF:(half + 1) * HALF, :]
                                 .bitcast(F32),
                                 mT[l * HALF:(l + 1) * HALF, half, :].bitcast(F32)
                                 ).then_inc(maxrow_in[half], 16)

            def step(j, par):
                if has(j + 1):
                    if has(j - 1):
                        lead(sp, CHUNKS * j)
                        sp.wait_ge(scores_ready, CHUNKS * j)
                    else:
                        sp.wait_ge(stacks_set, 1)
                        sp.wait_ge(mask_out, 16)
                        sp.wait_ge(hi_written, 32 * (j + 2))
                        sp.wait_ge(lo_written, 32 * (j + 2))
                    load_stack(1 - par, mask_dram[bass.ds(j + 1, 1), :], 1)
                if has(j):
                    load_max(par, 2 * j + 2, 1)
                if has(j + 2):
                    if has(j):
                        lead(sp, 80 * (j + 1), 2 * (j + 3), j + 3)
                        sp.wait_ge(stack_in[0], 80 * (j + 1))
                        sp.wait_ge(stack_in[1], 80 * (j + 1))
                    else:
                        lead(sp, 2 * (j + 3), j + 3)
                    for l, split, count, done in ((0, qk_hi, 2 * (j + 3), hi_written),
                                                  (1, qk_lo, j + 3, lo_written)):
                        sp.wait_ge(split, count)
                        for k in range(2):
                            sp.dma_start(scratch[par, k, l].rearrange("e p s -> p e s"),
                                         parts[:, k, l, :, :].bitcast(F32)).then_inc(done, 16)
                if has(j + 1):
                    load_max(1 - par, 2 * j + 3, 0)
                if has(j + 2):
                    lead(sp, 32 * (j + 3))
                    sp.wait_ge(hi_written, 32 * (j + 3))
                    sp.wait_ge(lo_written, 32 * (j + 3))
                    if has(j):
                        lead(sp, CHUNKS * j + CHUNKS // 2)
                        sp.wait_ge(scores_ready, CHUNKS * j + CHUNKS // 2)
                    else:
                        sp.wait_ge(stacks_set, 1)
                        sp.wait_ge(mask_out, 16)
                    load_stack(par, mask_dram[bass.ds(j + 2, 1), :], 0)

            steps(sp, step)
            for t in range(NBLK):
                for b in range(2):
                    sp.wait_ge(y_added, 2 * t + b + 1)
                    sp.dma_start(out_d[2 * t + b].rearrange("(t p) c -> p t c", p=P),
                                 y_sb[:, b * TT:(b + 1) * TT, :]).then_inc(out_written[b], 16)
            for b in range(2):
                sp.wait_ge(out_written[b], 16 * NBLK)

        @block.gpsimd
        def _(pool):
            pool.sem_inc(a_lo, 1)
            pool.memset(qs[0:64, :, :, :].bitcast(F32), 1.0)
            pool.memset(ks[0:64, :, :, :].bitcast(F32), -1.0).then_inc(stacks_set, 1)
            pool.memset(v_ones[:], 0.0).then_inc(v_ones_set, 1)
            pool.memset(minus_half[:], -0.5).then_inc(half_set, 1)

            def split_weights(n):
                cols = slice(n * W_CHUNK, (n + 1) * W_CHUNK)
                pool.wait_ge(w_in, 16 * (n - 1))
                pool.tensor_copy(wts[:, 0, cols], stage[:]).then_inc(w_hi, 1)
                pool.wait_ge(w_hi, n - 1)
                pool.tensor_tensor(wts[:, 1, cols], stage[:], wts[:, 0, cols].bitcast(F32),
                                   ALU.subtract).then_inc(w_split, 1)

            def inverse_deviation(n, count):
                pool.wait_ge(var_ready, count)
                pool.tensor_tensor(rstd[:, 0:n], var_eps[:, 0:n], minus_half[:, 0:n],
                                   ALU.pow).then_inc(rstd_ready, 1)

            def prepare_norm2(t):
                wait(pool, xn2_ready, t)
                inverse_deviation(BT, B + t + 1)
                pool.wait_ge(xn2_ready, t + 1)
                rows = x_sb[:, t * BT:(t + 1) * BT, :]
                pool.tensor_tensor(rows, rows, bff2_bc[:].unsqueeze(1).to_broadcast([P, BT, H]),
                                   ALU.add).then_inc(bff2_added, 1)

            def split_norm2(t):
                pool.wait_ge(h2_copied, t + 1)
                pool.wait_ge(scores_ready, CHUNKS * (B if t >= NBLK // 2 else B - 1))
                pool.tensor_copy(h2s[:, t, 0, :, :], h2_32).then_inc(h2_hi, 1)
                pool.wait_ge(h2_hi, t + 1)
                pool.tensor_tensor(h2s[:, t, 1, :, :], h2_32, h2s[:, t, 0, :, :].bitcast(F32),
                                   ALU.subtract).then_inc(h2_lo, 1)

            def step(j, par):
                if has(j + 3):
                    if at(j, -3):
                        pool.wait_ge(half_set, 1)
                    else:
                        pool.wait_ge(xn_ready, j + 3)
                    inverse_deviation(TT, j + 4)
                if has(j + 2):
                    pool.wait_ge(qk_hi, 2 * (j + 3))
                    wait(pool, lo_written, 32 * (j + 2))
                    pool.tensor_tensor(parts[:, :, 1, :, :].rearrange("p k e s -> p e k s"),
                                       rcos[:, :, :].rearrange("p (e k) s -> p e k s", e=2),
                                       parts[:, :, 0, :, :].bitcast(F32).rearrange("p k e s -> p e k s"),
                                       ALU.subtract).then_inc(qk_lo, 1)
                if has(j + 3):
                    pool.wait_ge(xn_ready, j + 4)
                    if at(j, -3):
                        pool.wait_ge(small_in, 16 * 7)
                    rows = x_sb[:, bass.ds((j + 3) * TT, TT), :]
                    pool.tensor_tensor(rows, rows, bo_bc[:].unsqueeze(1).to_broadcast([P, TT, H]),
                                       ALU.add).then_inc(bo_added, 1)
                if at(j, -3, -2, -1, 0):
                    split_weights(2 + j + 3)
                if has(j + 1):
                    if at(j, -1):
                        pool.wait_ge(v_ones_set, 1)
                    pool.wait_ge(mask_ready, 2)
                    pool.wait_ge(v_copied, j + 2)
                    wait(pool, pv_done, SLOTS * j)
                    seq = v_all[:, bass.ds((j + 1) % 4, 1), :, :].rearrange("p a t c -> p (a t) c")
                    pool.tensor_copy(v_ones[:, 1 - par, :, :, 0:HD],
                                     seq.rearrange("p t (h d) -> p t h d", d=HD))
                    m = mask_col[:, bass.ds((j + 1) * TT, TT)]
                    pool.tensor_copy(v_ones[:, 1 - par, :, :, HD:HD + 1],
                                     m.unsqueeze(2).unsqueeze(3).to_broadcast([P, TT, NH, 1])
                                     ).then_inc(v_ones_ready, 1)
                if at(j, B - 1, B):
                    prepare_norm2(j - (B - 1))
                if has(j - 1):
                    pool.wait_ge(a_hi, j)
                    pool.tensor_tensor(a_s[:, 1, :, :], aT32[:], a_s[:, 0, :, :].bitcast(F32),
                                       ALU.subtract).then_inc(a_lo, 1)
                if has(j + 3):
                    for e in range(2):
                        pool.wait_ge(qk_copied, 2 * (j + 3) + e + 1)
                        pool.tensor_tensor(rsin[:, 2 * e:2 * e + 2, :], qk32[:, 2 * e:2 * e + 2, :],
                                           rope[:, 1:2, :].to_broadcast([P, 2, S]),
                                           ALU.mult).then_inc(sin_done, 1)
                    pool.wait_ge(sin_done, 2 * (j + 4))
                    pool.wait_ge(cos_done, 2 * (j + 4))
                    pool.tensor_tensor(rcos[:, 2:4, :], rcos[:, 2:4, :], rsin[:, 0:2, :],
                                       ALU.add).then_inc(odd_rotated, 1)
                    pool.tensor_tensor(rcos[:, 0:2, :], rcos[:, 0:2, :], rsin[:, 2:4, :],
                                       ALU.subtract).then_inc(even_rotated, 1)

            steps(pool, step)
            split_norm2(1)
            for t in range(2, NBLK):
                prepare_norm2(t)
                split_norm2(t)

        @block.scalar
        def _(act):
            act.dma_start(x_sb[:, 0:TT, :], x_d[0].rearrange("(t p) c -> p t c", p=P)).then_inc(x_in, 16)
            act.dma_start(stage[:], weights_d[:, 0:W_CHUNK]).then_inc(w_first_in, 16)
            act.dma_start(qk32[:, :, :].rearrange("p a s -> p (a s)"),
                          weights_d[:, W_CHUNK:2 * W_CHUNK]).then_inc(w_first_in, 16)

            def copy_max(seq, half):
                act.wait_ge(max_turned, 2 * seq + half + 1)
                wait(act, maxrow_in[half], 32 * seq)
                act.activation(mT[:, half, :], ps_m2[0:2 * HALF, BANK[f"max{half}"], 0:S], ACT.Copy).then_inc(max_copied, 1)

            def load_weights(n):
                if n == 2:
                    act.wait_ge(w_first, 2)
                else:
                    act.wait_ge(w_split, n - 2)
                act.dma_start(stage[:], weights_d[:, n * W_CHUNK:(n + 1) * W_CHUNK]).then_inc(w_in, 16)

            def copy_out(seq, g):
                act.wait_ge(pv_done, SLOTS * seq + 2 * g + 2)
                wait(act, o_turned, 2 * seq + g // 2)
                act.activation(oT[:, g, :], ps_o[:, 0:S], ACT.Copy).then_inc(o_copied, 1)

            def step(j, par):
                if at(j, -3, -2, -1, 0):
                    load_weights(2 + j + 3)
                for s in range(SLOTS):
                    if has(j):
                        wait(act, pv_done, SLOTS * j + s - 1)
                        for c in (2 * s, 2 * s + 1):
                            act.wait_ge(scores_ready, CHUNKS * j + c + 1)
                            at_head = 2 * (c % 2)
                            act.activation(pT[:, s % 2, at_head:at_head + 2, :], ps_sc[:, c % 3, :, :],
                                           ACT.Exp, scale=SCALE).then_inc(exp_done, 1)
                    if s == 0 and has(j - 1):
                        copy_out(j - 1, 3)
                    if s in (2, 4, 6) and has(j):
                        copy_out(j, s // 2 - 1)
                    if s == 1 and has(j + 2):
                        act.wait_ge(v_ready, j + 3)
                        wait(act, v_ones_ready, j - 1)
                        if at(j, -2):
                            act.wait_ge(mask_ready, 2)
                        for t in range(TT):
                            op = act.activation(
                                v_all[:, bass.ds((j + 2) % 4, 1), t, :].rearrange("p a c -> p (a c)"),
                                ps_m2[:, BANK["v"], t * H:(t + 1) * H], ACT.Copy,
                                scale=mask_col[:, bass.ds((j + 2) * TT + t, 1)])
                        op.then_inc(v_copied, 1)
                    if s == 1 and has(j + 2):
                        act.wait_ge(even_rotated, j + 3)
                        wait(act, hi_written, 32 * (j + 2))
                        act.activation(parts[:, :, 0, 0, :], rcos[:, 0:2, :], ACT.Copy).then_inc(qk_hi, 1)
                    if s == 1 and has(j):
                        copy_max(j, 1)
                    if s == 3 and has(j + 3):
                        act.wait_ge(xn_turned, j + 4)
                        if at(j, -3):
                            act.wait_ge(aff_ready, 2)
                            act.wait_ge(w_first, 2)
                        wait(act, cos_done, 2 * (j + 3))
                        wait(act, sin_done, 2 * (j + 3))
                        for c in range(CC):
                            op = act.activation(h32[:, c, :], ps_m2[:, BANK["xn"], c * S:(c + 1) * S], ACT.Identity,
                                                scale=aff[:, 0, 0, c, bass.ds(j + 3, 1)],
                                                bias=aff[:, 0, 1, c, bass.ds(j + 3, 1)])
                        op.then_inc(h_copied, 1)
                    if s == 4 and has(j - 1):
                        act.wait_ge(on_turned, j + 1)
                        wait(act, a_lo, j)
                        for c in range(CC):
                            op = act.activation(aT32[:, c, :], ps_m2[:, BANK["on"], c * S:(c + 1) * S], ACT.Identity,
                                                bias=vec("bv", c))
                        op.then_inc(a_copied, 1)
                    if s == 4 and has(j + 1):
                        copy_max(j + 1, 0)
                    if s in (5, 6) and has(j + 3):
                        e = s - 5
                        act.wait_ge(qk_ready, 2 * (j + 3) + e + 1)
                        if e == 0:
                            act.wait_ge(h_lo, j + 4)
                        for k in range(2):
                            op = act.activation(qk32[:, 2 * e + k, :], ps_m2[:, BANK[("qk_even", "qk_odd")[e]], k * S:(k + 1) * S],
                                                ACT.Identity, bias=vec("bqk", 2 * e + k))
                        op.then_inc(qk_copied, 1)
                    if at(j, B) and s in GELU_AHEAD:
                        gelu(GELU_AHEAD[s])

            def copy_norm2(t):
                act.wait_ge(xn2_turned, t + 1)
                act.wait_ge(h2_lo, t)
                for c in range(CC):
                    for b in range(2):
                        op = act.activation(h2_32[:, c, b * S:(b + 1) * S],
                                            ps_t[:, c, b * S:(b + 1) * S], ACT.Identity,
                                            scale=aff[:, 1, 0, c, bass.ds(2 * t + b, 1)],
                                            bias=aff[:, 1, 1, c, bass.ds(2 * t + b, 1)])
                op.then_inc(h2_copied, 1)

            def gelu(n):
                f = n % FC
                act.wait_ge(f_ready, n + 1)
                wait(act, g_lo, n - 1)
                act.activation(g32[:, n % 2, :], ps_f[:, n % 3, :], ACT.Gelu,
                               bias=vec("ff_b1", f)).then_inc(g_done, 1)
                wait(act, ff2_done, n - AHEAD + 1)
                act.activation(gs[:, n % AHEAD, 0, :], ps_f[:, n % 3, :], ACT.Gelu,
                               bias=vec("ff_b1", f)).then_inc(g_hi, 1)

            steps(act, step)
            for n in range(len(GELU_AHEAD), NBLK * FC):
                gelu(n)
                if n % FC == 3 and n // FC + 1 < NBLK:
                    copy_norm2(n // FC + 1)

        @block.vector
        def _(dve):
            dve.wait_ge(small_in, 16 * 7)
            dve.tensor_copy(mask_col[:], mask_u8[:]).then_inc(mask_ready, 1)
            dve.tensor_scalar(mask_row[:], mrow_u8[:], -1.0, MASKED, ALU.add, ALU.mult).then_inc(mask_ready, 1)
            dve.wait_ge(w_first_in, 32)
            first = (stage[:], qk32[:, :, :].rearrange("p a s -> p (a s)"))
            for n in range(2):
                dve.tensor_copy(wts[:, 0, n * W_CHUNK:(n + 1) * W_CHUNK], first[n]).then_inc(w_first_hi, 1)
            for n in range(2):
                cols = slice(n * W_CHUNK, (n + 1) * W_CHUNK)
                dve.wait_ge(w_first_hi, n + 1)
                dve.tensor_tensor(wts[:, 1, cols], first[n], wts[:, 0, cols].bitcast(F32),
                                  ALU.subtract).then_inc(w_first, 1)
            for n in range(2):
                dve.wait_ge(mod_ready, 1)
                first_col = VECS[f"ada{n + 1}_b"][0]
                dve.tensor_tensor(
                    ada_mod[:, n, :, :],
                    ps_m[:, n * 64:n * 64 + 2 * CC * B].rearrange("p (a b) -> p a b", b=B),
                    vecs[:, first_col:first_col + 2 * CC].unsqueeze(2).to_broadcast([P, 2 * CC, B]),
                    ALU.add).then_inc(mod_added, 1)
                dve.wait_ge(mod_added, n + 1)
                for c in range(CC):
                    dve.tensor_scalar(aff[:, n, 0, c, :], ada_mod[:, n, CC + c, :], 1.0,
                                      vec(f"ln{n + 1}_g", c), ALU.add, ALU.mult)
                    dve.tensor_scalar(aff[:, n, 1, c, :], ada_mod[:, n, CC + c, :], 1.0,
                                      vec(f"ln{n + 1}_b", c), ALU.add, ALU.mult).then_inc(aff_half, 1)
                dve.wait_ge(aff_half, CC * (n + 1))
                dve.tensor_tensor(aff[:, n, 1, :, :], aff[:, n, 1, :, :], ada_mod[:, n, 0:CC, :],
                                  ALU.add).then_inc(aff_ready, 1)

            def norm_stats(seq_tile, n, step_sem, count, rstd_before):
                for t in range(n):
                    op = dve.bn_stats(stats[:, t, :], x_sb[:, bass.ds(seq_tile + t, 1), :].rearrange(
                        "p a c -> p (a c)"))
                op.then_inc(step_sem, 1)
                lead(dve)
                dve.wait_ge(step_sem, count + 1)
                for t in range(n):
                    op = dve.bn_aggr(mv[:, t, :], stats[:, t, :])
                op.then_inc(step_sem, 1)
                dve.wait_ge(step_sem, count + 2)
                wait(dve, rstd_ready, rstd_before)
                dve.tensor_scalar(var_eps[:, 0:n], mv[:, 0:n, 1:2].rearrange("p n a -> p (n a)"),
                                  EPS, None, ALU.add).then_inc(var_ready, 1)

            def norm_rows(rows, seq_tile, n, rstd_count, ready):
                dve.wait_ge(rstd_ready, rstd_count)
                for t in range(n):
                    op = dve.tensor_scalar(rows[:, t, :], x_sb[:, bass.ds(seq_tile + t, 1), :].rearrange(
                        "p a c -> p (a c)"), mv[:, t, 0:1], rstd[:, t:t + 1], ALU.subtract, ALU.mult)
                op.then_inc(ready, 1)

            def split_max(seq, half):
                dve.wait_ge(max_taken, NH * seq + HALF * (half + 1))
                wait(dve, max_turned, 2 * (seq - 1) + half + 1)
                dve.tensor_copy(mparts[:, half, :, 0, :].bitcast(F32R), m32[:, half, :, :]).then_inc(max_hi, 1)
                dve.wait_ge(max_hi, 2 * seq + half + 1)
                dve.tensor_tensor(mparts[:, half, :, 1, :], m32[:, half, :, :], mparts[:, half, :, 0, :],
                                  ALU.subtract).then_inc(max_lo, 1)

            def normalise(seq, pair):
                bank = ps_m2[:, BANK[f"o{pair}"], :]
                dve.wait_ge(o_turned, 2 * seq + pair + 2)
                dve.reciprocal(rden[:], bank.rearrange("p (n d) -> p n d", d=2 * HD)[:, :, HD:HD + 1]
                               .rearrange("p n a -> p (n a)")).then_inc(den_done, 1)
                dve.wait_ge(den_done, 2 * seq + pair + 1)
                wait(dve, on_turned, seq + 1)
                num = bank.rearrange("p (g t j d) -> p g t j d", g=2, t=TT, j=G4)
                den = rden[:].rearrange("p (g t j) -> p g t j", g=2, t=TT)
                for t in range(TT):
                    op = dve.tensor_tensor(
                        o_n[:, t, pair * P:(pair + 1) * P].rearrange("p (g j d) -> p g j d", g=2, j=G4),
                        num[:, :, t, :, 0:HD],
                        den[:, :, t, :].unsqueeze(3).to_broadcast([P, 2, G4, HD]), ALU.mult)
                op.then_inc(o_normed, 1)

            def take_max(seq, h):
                dve.wait_ge(max_scores, NH * seq + h + 1)
                if h % HALF == 0:
                    wait(dve, max_lo, 2 * (seq - 1) + h // HALF + 1)
                dve.tensor_reduce(
                    m32[:, h // HALF, :, h % HALF:h % HALF + 1].rearrange("p t a -> p (t a)"),
                    ps_max[:, h % 2, :].rearrange("p (t n) -> p t n", t=TT),
                    AX_X, ALU.max).then_inc(max_taken, 1)

            def split_gelu(n):
                dve.wait_ge(g_done, n + 1)
                dve.wait_ge(g_hi, n + 1)
                dve.tensor_tensor(gs[:, n % AHEAD, 1, :], g32[:, n % 2, :],
                                  gs[:, n % AHEAD, 0, :].bitcast(F32), ALU.subtract).then_inc(g_lo, 1)

            def step(j, par):
                for s in range(SLOTS):
                    if has(j + 1):
                        take_max(j + 1, 2 * s)
                        take_max(j + 1, 2 * s + 1)
                    if s == 0 and has(j + 3):
                        if at(j, -3):
                            dve.wait_ge(x_in, 16 * B)
                        norm_stats((j + 3) * TT, TT, norm_step, 2 * (j + 3), j + 3)
                    if s == 1 and has(j + 3):
                        wait(dve, xn_turned, j + 3)
                        norm_rows(xn, (j + 3) * TT, TT, j + 4, xn_ready)
                    if s == 1 and has(j + 2):
                        dve.wait_ge(odd_rotated, j + 3)
                        wait(dve, hi_written, 32 * (j + 2))
                        dve.tensor_copy(parts[:, :, 0, 1, :], rcos[:, 2:4, :]).then_inc(qk_hi, 1)
                    if s == 2 and has(j - 1):
                        normalise(j - 1, 1)
                    if s == 0 and at(j, B):
                        norm_stats(BT, BT, n2_step, 2, B + 1)
                    if s == 2 and at(j, B):
                        dve.wait_ge(xn2_turned, 1)
                        norm_rows(xn2, BT, BT, B + 2, xn2_ready)
                    if s == 0 and at(j, B - 1):
                        norm_stats(0, BT, n2_step, 0, B)
                    if s == 3 and at(j, B - 1):
                        dve.wait_ge(v_ones_ready, B)
                        norm_rows(xn2, 0, BT, B + 1, xn2_ready)
                    if s == 6 and at(j, B - 1):
                        dve.wait_ge(xn2_turned, 1)
                        dve.wait_ge(qk_lo, B)
                        for c in range(CC):
                            for b in range(2):
                                op = dve.tensor_scalar(h2_32[:, c, b * S:(b + 1) * S], ps_t[:, c, b * S:(b + 1) * S],
                                                       aff[:, 1, 0, c, b:b + 1], aff[:, 1, 1, c, b:b + 1],
                                                       ALU.mult, ALU.add)
                        op.then_inc(h2_copied, 1)
                        dve.wait_ge(h2_copied, 1)
                        dve.wait_ge(scores_ready, CHUNKS * (B - 1))
                        dve.tensor_copy(h2s[:, 0, 0, :, :], h2_32).then_inc(h2_hi, 1)
                        dve.wait_ge(h2_hi, 1)
                        dve.tensor_tensor(h2s[:, 0, 1, :, :], h2_32, h2s[:, 0, 0, :, :].bitcast(F32),
                                          ALU.subtract).then_inc(h2_lo, 1)
                    if s == 4 and has(j + 3):
                        dve.wait_ge(h_copied, j + 4)
                        wait(dve, v_ready, j + 3)
                        dve.tensor_copy(hs[:, 0, :, :], h32).then_inc(h_hi, 1)
                        dve.wait_ge(h_hi, j + 4)
                        dve.tensor_tensor(hs[:, 1, :, :], h32, hs[:, 0, :, :].bitcast(F32),
                                          ALU.subtract).then_inc(h_lo, 1)
                    if s == 3 and has(j + 1):
                        split_max(j + 1, 0)
                    if s == 7 and has(j - 1):
                        dve.wait_ge(attn_ready, j + 1)
                        dve.wait_ge(bo_added, j)
                        rows = x_sb[:, bass.ds((j - 1) * TT, TT), :]
                        dve.tensor_tensor(rows, ps_m2[:, BANK["proj_o"], :].rearrange("p (t c) -> p t c", t=TT), rows,
                                          ALU.add).then_inc(attn_added, 1)
                    if s == 5 and has(j - 1):
                        dve.wait_ge(a_copied, j)
                        wait(dve, attn_ready, j)
                        dve.tensor_copy(a_s[:, 0, :, :], aT32[:]).then_inc(a_hi, 1)
                    if s == 5 and has(j):
                        normalise(j, 0)
                    if s in (6, 7) and has(j + 3):
                        e = s - 6
                        dve.wait_ge(qk_copied, 2 * (j + 3) + e + 1)
                        wait(dve, qk_lo, j + 3)
                        dve.tensor_tensor(rcos[:, 2 * e:2 * e + 2, :], qk32[:, 2 * e:2 * e + 2, :],
                                          rope[:, 0:1, :].to_broadcast([P, 2, S]), ALU.mult).then_inc(cos_done, 1)
                    if s == 7 and has(j + 1):
                        split_max(j + 1, 1)
                    if at(j, B) and s in LO_AHEAD:
                        split_gelu(LO_AHEAD[s])

            steps(dve, step)

            def add_residual(t):
                for b in range(2):
                    if b == 0:
                        dve.wait_ge(y_ready, t + 1)
                    else:
                        dve.wait_ge(ff2_done, (t + 1) * FC)
                    dve.wait_ge(bff2_added, t + 1)
                    wait(dve, out_written[b], 16 * t)
                    dve.tensor_tensor(y_sb[:, b * TT:(b + 1) * TT, :], ps_y[:, b * TT:(b + 1) * TT, :],
                                      x_sb[:, t * BT + b * TT:t * BT + (b + 1) * TT, :],
                                      ALU.add).then_inc(y_added, 1)

            for n in range(len(LO_AHEAD), NBLK * FC):
                t, f = n // FC, n % FC
                split_gelu(n)
                if f == 2 and t > 0:
                    add_residual(t - 1)
                k = (n + 9) // FC
                if 2 <= k < NBLK and n == 8 * k - 9:
                    dve.wait_ge(attn_added, (k + 1) * BT // TT)
                    norm_stats(k * BT, BT, n2_step, 2 * k, B + k)
                if 2 <= k < NBLK and n == 8 * k - 8:
                    dve.wait_ge(xn2_turned, k)
                    norm_rows(xn2, k * BT, BT, B + k + 1, xn2_ready)
            add_residual(NBLK - 1)

        @block.tensor
        def _(pe):
            for free in (o_turned, on_turned, attn_ready):
                pe.sem_inc(free, 1)
            pe.wait_ge(cond_in, 16)
            pe.wait_ge(ada_in, 16)
            ada = pT[:, :, :, :].rearrange("p a g s -> p (a g s)").rearrange(
                "p (n c m) -> p n c m", n=2, c=CC)
            for n in range(2):
                for m in range(2 * CC):
                    for c in range(CC):
                        op = pe.matmul(ps_m[:, n * 64 + m * B:n * 64 + (m + 1) * B],
                                       ada[:, n, c, m * P:(m + 1) * P], condT[:, c, :],
                                       start=(c == 0), stop=(c == CC - 1))
            op.then_inc(mod_ready, 1)
            pe.wait_ge(small_in, 16 * 7)

            def w(l, col, n):
                return wts[:, l, col:col + n]

            def score_max(seq, par, h):
                if h % HALF == 0:
                    pe.wait_ge(stack_in[h // HALF], 80 * (seq + 1))
                wait(pe, max_taken, NH * seq + h - 1)
                for t in range(TT):
                    op = pe.matmul(ps_max[:, h % 2, t * S:(t + 1) * S],
                                   qs[0:ROWS_A, par, h, t * P:(t + 1) * P], ks[0:ROWS_A, par, h, :],
                                   start=True, stop=True)
                op.then_inc(max_scores, 1)

            def score_exp(seq, par, s):
                g, kt = s // 2, s % 2
                if s % (SLOTS // 2) == 0:
                    pe.wait_ge(maxrow_in[s // (SLOTS // 2)], 32 * (seq + 1))
                for c in (2 * s, 2 * s + 1):
                    wait(pe, exp_done, CHUNKS * seq + (c - 2 if c >= 3 else {0: 0, 1: -2, 2: -1}[c]))
                    for i in range(2):
                        h = g * G4 + 2 * (c % 2) + i
                        op = pe.matmul(ps_sc[:, c % 3, i, :], ks[0:ROWS_B, par, h, kt * P:(kt + 1) * P],
                                       qs[0:ROWS_B, par, h, :], start=True, stop=True)
                    op.then_inc(scores_ready, 1)

            def times_v(seq, par, s):
                g, kt = s // 2, s % 2
                if s == 0:
                    pe.wait_ge(v_ones_ready, seq + 1)
                pe.wait_ge(exp_done, CHUNKS * seq + 2 * s + 2)
                if kt == 0:
                    wait(pe, o_copied, NH // G4 * seq + g)
                for i in range(G4):
                    op = pe.matmul(ps_o[i * 32:(i + 1) * 32, 0:S], v_ones[:, par, kt, g * G4 + i, :],
                                   pT[:, s % 2, i, :], start=(kt == 0), stop=(kt == TT - 1))
                op.then_inc(pv_done, 1)

            def turn_max(seq, half):
                pe.wait_ge(max_lo, 2 * seq + half + 1)
                for t in range(TT):
                    op = pe.transpose(ps_m2[0:2 * HALF, BANK[f"max{half}"], t * P:(t + 1) * P],
                                      mparts[:, half, t, :, :].rearrange("p l h -> p (l h)"), ident[:])
                op.then_inc(max_turned, 1)

            def turn_out(seq, pair):
                pe.wait_ge(o_copied, NH // G4 * seq + 2 * pair + 2)
                for g in range(2):
                    for t in range(TT):
                        col = (g * TT + t) * P
                        op = pe.transpose(ps_m2[:, BANK[f"o{pair}"], col:col + P], oT[:, 2 * pair + g, t * P:(t + 1) * P], ident[:])
                op.then_inc(o_turned, 1)

            def turn_rows(src, name, done):
                for c in range(CC):
                    for t in range(TT):
                        op = pe.transpose(ps_m2[:, BANK[name], c * S + t * P:c * S + (t + 1) * P],
                                          src[:, t, c * P:(c + 1) * P], ident[:])
                op.then_inc(done, 1)

            def rows_times(acts, col, name, done):
                for t in range(TT):
                    for n, (lw, la) in enumerate(PARTS):
                        for c in range(CC):
                            op = pe.matmul(ps_m2[:, BANK[name], t * H:(t + 1) * H], acts[:, la, c, t * P:(t + 1) * P],
                                           w(lw, col + c * H, H), start=(n == 0 and c == 0),
                                           stop=(n == 2 and c == CC - 1))
                op.then_inc(done, 1)

            def misc(j, name):
                if name == "max1":
                    turn_max(j, 1)
                if name == "max0":
                    turn_max(j + 1, 0)
                if name == "o1":
                    turn_out(j - 1, 1)
                if name == "o0":
                    turn_out(j, 0)
                if name == "on":
                    pe.wait_ge(o_normed, 2 * j)
                    turn_rows(o_n, name, on_turned)
                if name == "xn":
                    pe.wait_ge(xn_ready, j + 4)
                    turn_rows(xn, name, xn_turned)
                if name == "proj_o":
                    pe.wait_ge(a_lo, j + 1)
                    rows_times(a_s, W_O, name, attn_ready)
                if name == "v":
                    rows_times(hs, W_V, name, v_ready)
                if name in ("qk_even", "qk_odd"):
                    e = 0 if name == "qk_even" else 1
                    if e == 0:
                        pe.wait_ge(h_hi, j + 4)
                        if at(j, -3):
                            pe.wait_ge(w_first, 2)
                    for n, k in ((0, 0), (1, 0), (0, 1), (1, 1), (2, 0), (2, 1)):
                        lw, la = PARTS[n]
                        if e == 0 and (n, k) == (2, 0):
                            pe.wait_ge(h_lo, j + 4)
                        for c in range(CC):
                            op = pe.matmul(ps_m2[:, BANK[name], k * S:(k + 1) * S],
                                           w(lw, W_QK + (c * 4 + 2 * e + k) * P, P), hs[:, la, c, :],
                                           start=(n == 0 and k == 0 and c == 0),
                                           stop=(n == 2 and c == CC - 1), skip_group_check=True)
                    op.then_inc(qk_ready, 1)

            def step(j, par):
                def turns(place):
                    for index, (where, name, off, _, _, _) in enumerate(MISC):
                        if where == place and has(j + off):
                            wait_bank(pe, j, index)
                            misc(j, name)

                for s in range(SLOTS):
                    if has(j):
                        score_exp(j, par, s)
                    turns(EARLY + s)
                    if s == 5 and at(j, B - 1):
                        turn_norm2(0)
                    if at(j, B) and s in FF1_AHEAD:
                        ff1(FF1_AHEAD[s])
                    if at(j, B) and s == 6:
                        turn_norm2(1)
                    if has(j + 1):
                        score_max(j + 1, 1 - par, 2 * s)
                        score_max(j + 1, 1 - par, 2 * s + 1)
                    if s == 0 and has(j - 1):
                        times_v(j - 1, 1 - par, SLOTS - 1)
                    if s > 0 and has(j):
                        times_v(j, par, s - 1)
                    turns(s)

            def turn_norm2(t):
                pe.wait_ge(xn2_ready, t + 1)
                if t == 0:
                    pe.wait_ge(max_taken, NH * B)
                else:
                    pe.wait_ge(h2_copied, t)
                for c in range(CC):
                    for i in range(BT):
                        op = pe.transpose(ps_t[:, c, i * P:(i + 1) * P], xn2[:, i, c * P:(c + 1) * P], ident[:])
                op.then_inc(xn2_turned, 1)

            def ff1(n):
                t, f = n // FC, n % FC
                if f == 0:
                    pe.wait_ge(h2_lo, t + 1)
                if n == 0:
                    pe.wait_ge(w_split, 4)
                if n < 3:
                    pe.wait_ge(exp_done, CHUNKS * B)
                else:
                    pe.wait_ge(g_hi, n - 2)
                for k, (lw, la) in enumerate(PARTS):
                    for c in range(CC):
                        op = pe.matmul(ps_f[:, n % 3, :], w(lw, W_1 + c * FF + f * P, P), h2s[:, t, la, c, :],
                                       start=(k == 0 and c == 0), stop=(k == 2 and c == CC - 1))
                op.then_inc(f_ready, 1)

            def ff2(n):
                t, f = n // FC, n % FC
                pe.wait_ge(g_lo, n + 1)
                for i in range(BT):
                    if f == 0 and i % 2 == 0:
                        if t == 0:
                            pe.wait_ge(attn_added, B)
                        else:
                            pe.wait_ge(y_added, 2 * (t - 1) + i // 2 + 1)
                    for k, (lw, la) in enumerate(PARTS):
                        op = pe.matmul(ps_y[:, i, :], gs[:, n % AHEAD, la, i * P:(i + 1) * P],
                                       w(lw, W_2 + f * H, H), start=(f == 0 and k == 0 and i % 2 == 0),
                                       stop=(f == FC - 1 and k == 2), skip_group_check=True)
                    if f == FC - 1 and i == 1:
                        op.then_inc(y_ready, 1)
                op.then_inc(ff2_done, 1)

            steps(pe, step)
            for n in range(NBLK * FC):
                ff2(n)
                if n + AHEAD < NBLK * FC:
                    ff1(n + AHEAD)
                if n % FC == 6 and n // FC + 2 < NBLK:
                    turn_norm2(n // FC + 2)


def _chunks(a):
    c = a.shape[0] // P
    return a.reshape(c, P, -1).transpose(1, 0, 2).reshape(P, -1)


def kernel(**inputs):
    import numpy as np
    import concourse.bacc as bacc
    from concourse.bass_utils import run_bass_kernel_spmd

    a = {k.removeprefix("L0_cond_"): np.asarray(v) for k, v in inputs.items()}

    def rotary_columns(w, odd):
        return w.reshape(w.shape[0], NH, ROT, 2)[:, :, :, odd].transpose(0, 2, 1).reshape(w.shape[0], P)

    qk = np.concatenate([rotary_columns(a[n], odd) for odd in (0, 1) for n in ("wq", "wk")], axis=1)
    weights = np.concatenate([_chunks(w) for w in (qk, a["wv"], a["wo"], a["ff_w1"], a["ff_w2"])], axis=1)
    bqk = np.concatenate([rotary_columns(a[n][None], odd) for odd in (0, 1) for n in ("bq", "bk")], axis=0)
    vecs = np.concatenate([bqk.T] + [a[n].reshape(-1, P).T for n in (
        "bv", "ln1_g", "ln1_b", "ada1_b", "ln2_g", "ln2_b", "ada2_b", "ff_b1")], axis=1)
    inv = (np.float32(1.0) / np.power(np.float32(10000.0), np.arange(ROT, dtype=np.float32) / np.float32(ROT)))
    ang = np.arange(S, dtype=np.float32)[:, None] * inv.astype(np.float32)[None, :]
    rope = np.stack([np.cos(ang), np.sin(ang)]).transpose(2, 0, 1).astype(np.float32)
    arrays = {
        "x": a["x"],
        "condT": a["cond_1024"].reshape(B, CC, P).transpose(2, 1, 0),
        "mask_row": a["mask_BxS_bf1"].view(np.uint8),
        "mask_col": a["mask_BxS_bf1"].view(np.uint8).reshape(B * TT, P).T,
        "weights": weights,
        "ada": np.concatenate([_chunks(a["ada1_w"]), _chunks(a["ada2_w"])], axis=1),
        "vecs": vecs,
        "rope": np.repeat(rope, NH, axis=0),
        "bo": a["bo"],
        "bff2": a["ff_b2"],
        "ident": np.eye(P, dtype=np.float32),
    }
    arrays = {f"{k}_dram": np.ascontiguousarray(v) for k, v in arrays.items()}
    nc = bacc.Bacc("TRN2", target_bir_lowering=False, num_devices=1)
    args = [nc.dram_tensor(k, v.shape, mybir.dt.from_np(v.dtype), kind="ExternalInput").ap()
            for k, v in arrays.items()]
    out = nc.dram_tensor("out_dram", (B, S, H), F32, kind="ExternalOutput").ap()
    block_kernel(nc, *args, out)
    r = run_bass_kernel_spmd(nc, [arrays], core_ids=[0])
    return r.results[0]["out_dram"]
```

```python
from contextlib import ExitStack

import concourse.bass as bass
from concourse import mybir

ALU = mybir.AluOpType
ACT = mybir.ActivationFunctionType
F32 = mybir.dt.float32
F32R = mybir.dt.float32r
U8 = mybir.dt.uint8
AX_X = mybir.AxisListType.X

P = 128
B, S, H, NH = 8, 256, 256, 16
HD = H // NH
ROT = HD // 2
FF = 4 * H
CC = H // P
TT = S // P
FC = FF // P
EPS = 1e-5
SCALE = float(HD) ** -0.5
MASKED = 1e30
G4 = 4
CHUNKS = 2 * NH // 2
SLOTS = 2 * NH // G4
HALF = NH // 2

ROW_MASK = 3 * HD
ROWS_A = ROW_MASK + 1
ROW_MAX = ROWS_A
ROWS_B = ROW_MAX + 2

W_QK, W_V = 0, CC * 2 * H
W_O = W_V + CC * H
W_1 = W_O + CC * H
W_2 = W_1 + CC * FF
W_ALL = W_2 + FC * H
W_CHUNK = 1024

VECS = {}
_at = 0
for _name, _n in (("bqk", 4), ("bv", CC), ("ln1_g", CC), ("ln1_b", CC), ("ada1_b", 2 * CC),
                  ("ln2_g", CC), ("ln2_b", CC), ("ada2_b", 2 * CC), ("ff_b1", FC)):
    VECS[_name] = (_at, _n)
    _at += _n
N_VEC = _at

PARTS = ((0, 0), (1, 0), (0, 1))


def block_kernel(nc, x_d, condT_d, mask_row_d, mask_col_d, weights_d, ada_d, vecs_d, rope_d,
                 bo_d, bff2_d, ident_d, out_d):
    ctx = ExitStack()
    with ctx:
        def sb(name, shape, dt=F32):
            return ctx.enter_context(nc.sbuf_tensor(name, shape, dt))

        def ps(name, shape):
            return ctx.enter_context(nc.psum_tensor(name, shape, F32))

        def sem(name):
            return ctx.enter_context(nc.semaphore(name))

        x_sb = sb("x_sb", [P, B * TT, H])
        wts = sb("wts", [P, 2, W_ALL], F32R)
        stage = sb("stage", [P, W_CHUNK])
        vecs = sb("vecs", [P, N_VEC])
        rope = sb("rope", [P, 2, S])
        ident = sb("ident", [P, P])
        bo_bc = sb("bo_bc", [P, H])
        bff2_bc = sb("bff2_bc", [P, H])
        condT = sb("condT", [P, CC, B])
        ada_mod = sb("ada_mod", [P, 2, 2 * CC, B])
        aff = sb("aff", [P, 2, 2, CC, B])
        mask_u8 = sb("mask_u8", [P, B * TT], U8)
        mask_col = sb("mask_col", [P, B * TT])
        mrow_u8 = sb("mrow_u8", [B, S], U8)
        mask_row = sb("mask_row", [B, S], F32R)
        ones = sb("ones", [1, 2, S], F32R)
        stats = sb("stats", [P, 4, 6])
        mv = sb("mv", [P, 4, 2])
        var_eps = sb("var_eps", [P, 4])
        minus_half = sb("minus_half", [P, 4])
        rstd = sb("rstd", [P, 4])
        rows_n = sb("rows_n", [P, 4, H])
        hs = sb("hs", [P, 2, CC, S], F32R)
        qk32 = sb("qk32", [P, 4, S])
        h32 = qk32[:, 0:CC, :]
        rcos = sb("rcos", [P, 4, S])
        rsin = sb("rsin", [P, 4, S])
        parts = sb("parts", [P, 2, 2, 2, S], F32R)
        qs = sb("qs", [P, 2, NH, S], F32R)
        ks = sb("ks", [P, 2, NH, S], F32R)
        v_all = sb("v_all", [P, 4, TT, H])
        v_ones = sb("v_ones", [P, 2, TT, NH, 2 * HD])
        m32 = sb("m32", [P, 2, TT, HALF])
        mparts = sb("mparts", [P, 2, TT, 2, HALF])
        mT = sb("mT", [2 * HALF, 2, S], F32R)
        pT = sb("pT", [P, 2, G4, S])
        oT = sb("oT", [P, NH // G4, S])
        rden = sb("rden", [P, 2 * TT * G4])
        xn = rows_n
        o_n = rows_n[:, TT:2 * TT, :]
        aT32 = sb("aT32", [P, CC, S])
        a_s = sb("a_s", [P, 2, CC, S], F32R)

        ps_max = ps("ps_max", [P, 2, 512])
        ps_sc = ps("ps_sc", [P, 3, 2, S])
        ps_o = ps("ps_o", [P, 512])
        ps_m2 = ps("ps_m", [P, 2, 512])
        ps_mod = (ps_sc[:, 0, 0, 0:2 * CC * B], ps_sc[:, 1, 0, 0:2 * CC * B])

        scratch = nc.dram_tensor("scratch", [2, 2, 2, 2, P, S], F32, kind="Internal").ap()
        mask_dram = nc.dram_tensor("mask_dram", [B, S], F32, kind="Internal").ap()

        BT = 4
        NBLK = B * TT // BT
        TB = BT * P
        h2s = qs[:, :, :, :].rearrange("p a h s -> p (a h s)").rearrange(
            "p (t l c n) -> p t l c n", t=NBLK, l=2, c=CC)
        mlp_room = ks[:, :, :, :].rearrange("p a h s -> p (a h s)")
        AHEAD = 4
        FF1_AHEAD = {1: 0, 3: 1, 4: 2, 5: 3}
        GELU_AHEAD = {2: 0, 4: 1, 5: 2}
        LO_AHEAD = {3: 0, 5: 1}
        gs = mlp_room[:, 0:AHEAD * 2 * TB].rearrange("p (f l n) -> p f l n", f=AHEAD, l=2)
        h2_32 = rcos[:, :, :].rearrange("p a s -> p (a s)").rearrange("p (c n) -> p c n", c=CC)
        g32 = rsin[:, :, :].rearrange("p a s -> p (a s)").rearrange("p (f n) -> p f n", f=2)
        y_sb = qk32[:, :, :]
        ps_t = ps_max
        ps_f = ps_sc[:, :, :, :].rearrange("p f a s -> p f (a s)")
        xn2 = v_all[:, 0:BT // TT, :, :].rearrange("p a t c -> p (a t) c")
        ps_y = ps_m2[:, :, :].rearrange("p a (i c) -> p (a i) c", i=2)

        cond_in, x_in, small_in, bff2_in = sem("cond_in"), sem("x_in"), sem("small_in"), sem("bff2_in")
        x_first_in, ident_in, vecs_in, ada_in = (
            sem("x_first_in"), sem("ident_in"), sem("vecs_in"), [sem("ada1_in"), sem("ada2_in")])
        w_in, w_hi, w_split = sem("w_in"), sem("w_hi"), sem("w_split")
        w_first_in, w_first_hi, w_first = [sem("w_qk_in"), sem("w_vo_in")], sem("w_first_hi"), sem("w_first")
        stacks_set, v_ones_set, half_set, ones_set = (
            sem("stacks_set"), sem("v_ones_set"), sem("half_set"), sem("ones_set"))
        mask_ready, mask_out, mod_ready, mod_added, aff_half, aff_ready = (
            sem("mask_ready"), sem("mask_out"), sem("mod_ready"), sem("mod_added"), sem("aff_half"), sem("aff_ready"))
        norm_step, xn_ready, xn_turned, h_copied, h_hi, h_lo = (
            sem("norm_step"), sem("xn_ready"), sem("xn_turned"), sem("h_copied"), sem("h_hi"), sem("h_lo"))
        bo_added = sem("bo_added")
        qk_ready, qk_copied, v_ready, v_copied, v_ones_ready = (
            sem("qk_ready"), sem("qk_copied"), sem("v_ready"), sem("v_copied"), sem("v_ones_ready"))
        cos_done, sin_done, even_rotated, odd_rotated, qk_hi, qk_lo = (
            sem("cos_done"), sem("sin_done"), sem("even_rotated"), sem("odd_rotated"), sem("qk_hi"), sem("qk_lo"))
        hi_written, lo_written = sem("hi_written"), sem("lo_written")
        stack_in = [sem("stack_in0"), sem("stack_in1")]
        maxrow_in = [sem("maxrow_in0"), sem("maxrow_in1")]
        max_scores, max_taken, max_hi, max_lo, max_turned, max_copied = (
            sem("max_scores"), sem("max_taken"), sem("max_hi"), sem("max_lo"), sem("max_turned"), sem("max_copied"))
        scores_ready, exp_done, pv_done, o_copied, o_turned = (
            sem("scores_ready"), sem("exp_done"), sem("pv_done"), sem("o_copied"), sem("o_turned"))
        den_done, o_normed, on_turned, a_copied, a_hi, a_lo, attn_ready, attn_added = (
            sem("den_done"), sem("o_normed"), sem("on_turned"), sem("a_copied"), sem("a_hi"), sem("a_lo"),
            sem("attn_ready"), sem("attn_added"))
        var_ready, rstd_ready, n2_step, xn2_ready, xn2_turned, h2_copied, h2_hi, h2_lo, bff2_added = (
            sem("var_ready"), sem("rstd_ready"), sem("n2_step"), sem("xn2_ready"), sem("xn2_turned"),
            sem("h2_copied"), sem("h2_hi"), sem("h2_lo"),
            sem("bff2_added"))
        f_ready, g_done, g_hi, g_lo, ff2_done, y_ready, y_added, out_written = (
            sem("f_ready"), sem("g_done"), sem("g_hi"), sem("g_lo"), sem("ff2_done"), sem("y_ready"), sem("y_added"),
            [sem("out_written0"), sem("out_written1")])

        def wait(eng, s, value):
            if not isinstance(value, int) or value > 0:
                eng.wait_ge(s, value)

        def lead(eng, *counts):
            for count in counts:
                if not isinstance(count, int):
                    eng.compute_val(count)
            eng.wait_ge(half_set, 1)

        def has(seq):
            return not isinstance(seq, int) or 0 <= seq < B

        def at(j, *which):
            return isinstance(j, int) and j in which

        DVE_ROTATES = (-3, -2)
        DVE_SPLITS = (-2, B - 3)

        def weights_lo(eng, n):
            cols = slice(n * W_CHUNK, (n + 1) * W_CHUNK)
            eng.wait_ge(w_hi, n - 1)
            eng.tensor_tensor(wts[:, 1, cols], stage[:], wts[:, 0, cols].bitcast(F32),
                              ALU.subtract).then_inc(w_split, 1)

        def rotate_even(eng):
            eng.tensor_tensor(rcos[:, 0:2, :], rcos[:, 0:2, :], rsin[:, 2:4, :],
                              ALU.subtract).then_inc(even_rotated, 1)

        def qk_lo_part(eng, seq):
            eng.wait_ge(qk_hi, 2 * (seq + 1))
            wait(eng, lo_written, 32 * seq)
            eng.tensor_tensor(parts[:, :, 1, :, :].rearrange("p k e s -> p e k s"),
                              rcos[:, :, :].rearrange("p (e k) s -> p e k s", e=2),
                              parts[:, :, 0, :, :].bitcast(F32).rearrange("p k e s -> p e k s"),
                              ALU.subtract).then_inc(qk_lo, 1)

        LN_EARLY = (-2, -1, 0)

        def steps(eng, step):
            for j in range(-3, 1):
                step(j, j % 2)
            with eng.Fori(0, (B - 4) // 2) as i:
                step(2 * i + 1, 1)
                step(2 * i + 2, 0)
            for j in range(B - 3, B + 1):
                step(j, j % 2)

        def vec(name, k=0):
            col = VECS[name][0] + k
            return vecs[:, col:col + 1]

        EARLY = 100
        MISC = [
            (0, "v", 2, v_copied, 1, 1),
            (1, "max1", 0, max_copied, 2, 2),
            (EARLY + 2, "o1", -1, o_normed, 2, 2),
            (2, "xn", 3, h_copied, 1, 1),
            (3, "on", -1, a_copied, 1, 1),
            (4, "max0", 1, max_copied, 2, 1),
            (5, "qk_even", 3, qk_copied, 2, 1),
            (5, "o0", 0, o_normed, 2, 1),
            (6, "qk_odd", 3, qk_copied, 2, 2),
            (EARLY + 7, "proj_o", -1, attn_added, 1, 1),
        ]
        BANK = {name: n % 2 for n, (_, name, *_) in enumerate(MISC)}

        def bank(j, name):
            return BANK[name] ^ int(name == "qk_odd" and isinstance(j, int) and j < 0)

        def wait_bank(pe, j, index):
            mine = bank(j, MISC[index][1])
            n, jj = index - 1, j
            for _ in range(2 * len(MISC)):
                if n < 0:
                    n, jj = n + len(MISC), jj - 1
                _, name, off, s, per, which = MISC[n]
                if has(jj + off) and bank(jj, name) == mine:
                    pe.wait_ge(s, (jj + off) * per + which)
                    return
                n -= 1

        block = ctx.enter_context(nc.Block())

        @block.sync
        def _(sp):
            ada = pT[:, :, :, :].rearrange("p a g s -> p a (g s)")
            sp.dma_start(condT[:], condT_d).then_inc(cond_in, 16)
            sp.dma_start(ada[:, 0, :], ada_d[:, 0:G4 * S]).then_inc(ada_in[0], 16)
            sp.dma_start(ident[:], ident_d).then_inc(ident_in, 16)
            sp.dma_start(vecs[:], vecs_d).then_inc(vecs_in, 16)
            for to, frm in ((rope, rope_d), (mask_u8, mask_col_d), (mrow_u8, mask_row_d)):
                sp.dma_start(to[:], frm).then_inc(small_in, 16)
            sp.dma_start(bo_bc[:], bo_d.partition_broadcast(P)).then_inc(small_in, 16)
            for b in range(1, B):
                sp.dma_start(x_sb[:, b * TT:(b + 1) * TT, :],
                             x_d[b].rearrange("(t p) c -> p t c", p=P)).then_inc(x_in, 16)
                if b == 1:
                    sp.dma_start(ada[:, 1, :], ada_d[:, G4 * S:2 * G4 * S]).then_inc(ada_in[1], 16)
            sp.wait_ge(ones_set, 2)
            for par in range(2):
                for to, row, sign in ((qs, ROW_MASK, 0), (ks, ROW_MAX, 1), (ks, ROW_MAX + 1, 1)):
                    sp.dma_start(to[row:row + 1, par, :, :].bitcast(F32),
                                 ones[:, sign, :].bitcast(F32).unsqueeze(1).to_broadcast([1, NH, S])
                                 ).then_inc(stacks_set, 16)
            sp.dma_start(bff2_bc[:], bff2_d.partition_broadcast(P)).then_inc(bff2_in, 16)

            sp.wait_ge(mask_ready, 2)
            sp.dma_start(mask_dram, mask_row[:].bitcast(F32)).then_inc(mask_out, 16)

            def load_stack(par, mask, half):
                heads = slice(half * HALF, (half + 1) * HALF)
                for t, k, rows in ((qs, 0, ((0, 0, 2), (2, 0, 1))), (ks, 1, ((0, 0, 1), (1, 0, 2)))):
                    src = scratch[par, k].rearrange("l e (i h) s -> (l e i) h s", h=NH)
                    for to, frm, n in rows:
                        sp.dma_start(t[to * HD:(to + n) * HD, par, heads, :].bitcast(F32),
                                     src[frm * HD:(frm + n) * HD, heads, :]).then_inc(stack_in[half], 16)
                sp.dma_start(ks[ROW_MASK:ROW_MASK + 1, par, heads, :].bitcast(F32),
                             mask.unsqueeze(1).to_broadcast([1, HALF, S])).then_inc(stack_in[half], 16)

            def load_max(par, turned, half):
                lead(sp, turned)
                sp.wait_ge(max_copied, turned)
                for l in range(2):
                    sp.dma_start(qs[ROW_MAX + l:ROW_MAX + l + 1, par, half * HALF:(half + 1) * HALF, :]
                                 .bitcast(F32),
                                 mT[l * HALF:(l + 1) * HALF, half, :].bitcast(F32)
                                 ).then_inc(maxrow_in[half], 16)

            def step(j, par):
                if has(j + 1):
                    if has(j - 1):
                        lead(sp, CHUNKS * j)
                        sp.wait_ge(scores_ready, CHUNKS * j)
                    else:
                        sp.wait_ge(stacks_set, 96)
                        sp.wait_ge(mask_out, 16)
                        sp.wait_ge(hi_written, 32 * (j + 2))
                        sp.wait_ge(lo_written, 32 * (j + 2))
                    load_stack(1 - par, mask_dram[bass.ds(j + 1, 1), :], 1)
                if has(j):
                    load_max(par, 2 * j + 2, 1)
                if has(j + 2):
                    if has(j):
                        lead(sp, 80 * (j + 1), 2 * (j + 3), j + 3)
                        sp.wait_ge(stack_in[0], 80 * (j + 1))
                        sp.wait_ge(stack_in[1], 80 * (j + 1))
                    else:
                        lead(sp, 2 * (j + 3), j + 3)
                    for l, split, count, done in ((0, qk_hi, 2 * (j + 3), hi_written),
                                                  (1, qk_lo, j + 3, lo_written)):
                        sp.wait_ge(split, count)
                        for k in range(2):
                            sp.dma_start(scratch[par, k, l].rearrange("e p s -> p e s"),
                                         parts[:, k, l, :, :].bitcast(F32)).then_inc(done, 16)
                if has(j + 1):
                    load_max(1 - par, 2 * j + 3, 0)
                if has(j + 2):
                    lead(sp, 32 * (j + 3))
                    sp.wait_ge(hi_written, 32 * (j + 3))
                    sp.wait_ge(lo_written, 32 * (j + 3))
                    if has(j):
                        lead(sp, CHUNKS * j + CHUNKS // 2)
                        sp.wait_ge(scores_ready, CHUNKS * j + CHUNKS // 2)
                    else:
                        sp.wait_ge(stacks_set, 96)
                        sp.wait_ge(mask_out, 16)
                    load_stack(par, mask_dram[bass.ds(j + 2, 1), :], 0)

            steps(sp, step)
            for t in range(NBLK):
                for b in range(2):
                    sp.wait_ge(y_added, 2 * t + b + 1)
                    sp.dma_start(out_d[2 * t + b].rearrange("(t p) c -> p t c", p=P),
                                 y_sb[:, b * TT:(b + 1) * TT, :]).then_inc(out_written[b], 16)
            for b in range(2):
                sp.wait_ge(out_written[b], 16 * NBLK)

        @block.gpsimd
        def _(pool):
            pool.sem_inc(a_lo, 1)
            pool.memset(minus_half[:], -0.5).then_inc(half_set, 1)
            pool.memset(ones[:, 0, :].bitcast(F32), 1.0).then_inc(ones_set, 1)
            pool.memset(ones[:, 1, :].bitcast(F32), -1.0).then_inc(ones_set, 1)

            def inverse_deviation(n, count):
                pool.wait_ge(var_ready, count)
                pool.tensor_tensor(rstd[:, 0:n], var_eps[:, 0:n], minus_half[:, 0:n],
                                   ALU.pow).then_inc(rstd_ready, 1)

            def deviation_norm2(t):
                wait(pool, xn2_ready, t)
                inverse_deviation(BT, B + t + 1)

            def add_bff2(t):
                pool.wait_ge(xn2_ready, t + 1)
                if t == 0:
                    pool.wait_ge(bff2_in, 16)
                rows = x_sb[:, t * BT:(t + 1) * BT, :]
                pool.tensor_tensor(rows, rows, bff2_bc[:].unsqueeze(1).to_broadcast([P, BT, H]),
                                   ALU.add).then_inc(bff2_added, 1)

            def split_norm2(t):
                pool.wait_ge(h2_copied, t + 1)
                pool.wait_ge(scores_ready, CHUNKS * (B if t >= NBLK // 2 else B - 1))
                pool.tensor_copy(h2s[:, t, 0, :, :], h2_32).then_inc(h2_hi, 1)
                pool.wait_ge(h2_hi, t + 1)
                pool.tensor_tensor(h2s[:, t, 1, :, :], h2_32, h2s[:, t, 0, :, :].bitcast(F32),
                                   ALU.subtract).then_inc(h2_lo, 1)

            def step(j, par):
                if at(j, -3):
                    pool.wait_ge(half_set, 1)
                    inverse_deviation(TT, 1)
                    pool.memset(v_ones[:], 0.0).then_inc(v_ones_set, 1)
                elif has(j + 3) and not at(j, *LN_EARLY):
                    pool.wait_ge(xn_ready, j + 3)
                    inverse_deviation(TT, j + 4)
                if has(j + 2) and not at(j, *DVE_SPLITS):
                    qk_lo_part(pool, j + 2)
                if has(j + 3):
                    pool.wait_ge(xn_ready, j + 4)
                    if at(j, -3):
                        pool.wait_ge(small_in, 16 * 4)
                    rows = x_sb[:, bass.ds((j + 3) * TT, TT), :]
                    pool.tensor_tensor(rows, rows, bo_bc[:].unsqueeze(1).to_broadcast([P, TT, H]),
                                       ALU.add).then_inc(bo_added, 1)
                if at(j, -2, -1, 0):
                    weights_lo(pool, j + 4)
                if at(j + 1, *LN_EARLY):
                    pool.wait_ge(xn_ready, j + 4)
                    inverse_deviation(TT, j + 5)
                if has(j + 1):
                    if at(j, -1):
                        pool.wait_ge(v_ones_set, 1)
                    pool.wait_ge(mask_ready, 2)
                    pool.wait_ge(v_copied, j + 2)
                    wait(pool, pv_done, SLOTS * j)
                    seq = v_all[:, bass.ds((j + 1) % 4, 1), :, :].rearrange("p a t c -> p (a t) c")
                    pool.tensor_copy(v_ones[:, 1 - par, :, :, 0:HD],
                                     seq.rearrange("p t (h d) -> p t h d", d=HD))
                    m = mask_col[:, bass.ds((j + 1) * TT, TT)]
                    pool.tensor_copy(v_ones[:, 1 - par, :, :, HD:HD + 1],
                                     m.unsqueeze(2).unsqueeze(3).to_broadcast([P, TT, NH, 1])
                                     ).then_inc(v_ones_ready, 1)
                if at(j, B - 1):
                    deviation_norm2(0)
                    add_bff2(0)
                if has(j - 1):
                    pool.wait_ge(a_hi, j)
                    pool.tensor_tensor(a_s[:, 1, :, :], aT32[:], a_s[:, 0, :, :].bitcast(F32),
                                       ALU.subtract).then_inc(a_lo, 1)
                if at(j, B - 1):
                    deviation_norm2(1)
                if has(j + 3):
                    if at(j, -3):
                        pool.wait_ge(w_first, 2)
                    for e in range(2):
                        pool.wait_ge(qk_copied, 2 * (j + 3) + e + 1)
                        pool.tensor_tensor(rsin[:, 2 * e:2 * e + 2, :], qk32[:, 2 * e:2 * e + 2, :],
                                           rope[:, 1:2, :].to_broadcast([P, 2, S]),
                                           ALU.mult).then_inc(sin_done, 1)
                    pool.wait_ge(sin_done, 2 * (j + 4))
                    pool.wait_ge(cos_done, 2 * (j + 4))
                    pool.tensor_tensor(rcos[:, 2:4, :], rcos[:, 2:4, :], rsin[:, 0:2, :],
                                       ALU.add).then_inc(odd_rotated, 1)
                    if not at(j, *DVE_ROTATES):
                        rotate_even(pool)

            steps(pool, step)
            add_bff2(1)
            split_norm2(1)
            for t in range(2, NBLK):
                deviation_norm2(t)
                add_bff2(t)
                split_norm2(t)

        @block.scalar
        def _(act):
            act.dma_start(x_sb[:, 0:TT, :], x_d[0].rearrange("(t p) c -> p t c", p=P)).then_inc(x_first_in, 16)
            first = (stage[:], rsin[:, :, :].rearrange("p a s -> p (a s)"))
            for n in range(2):
                act.dma_start(first[n], weights_d[:, n * W_CHUNK:(n + 1) * W_CHUNK]).then_inc(w_first_in[n], 16)
            for n in range(2):
                act.wait_ge(w_first_in[n], 16)
                act.activation(wts[:, 0, n * W_CHUNK:(n + 1) * W_CHUNK], first[n], ACT.Copy).then_inc(w_first_hi, 1)

            def copy_max(seq, half):
                act.wait_ge(max_turned, 2 * seq + half + 1)
                wait(act, maxrow_in[half], 32 * seq)
                act.activation(mT[:, half, :], ps_m2[0:2 * HALF, BANK[f"max{half}"], 0:S], ACT.Copy).then_inc(max_copied, 1)

            def load_weights(n):
                if n == 2:
                    act.wait_ge(w_first, 1)
                else:
                    act.wait_ge(w_split, n - 2)
                act.dma_start(stage[:], weights_d[:, n * W_CHUNK:(n + 1) * W_CHUNK]).then_inc(w_in, 16)

            def weights_hi(n):
                act.wait_ge(w_in, 16 * (n - 1))
                act.activation(wts[:, 0, n * W_CHUNK:(n + 1) * W_CHUNK], stage[:], ACT.Copy).then_inc(w_hi, 1)

            def copy_out(seq, g):
                act.wait_ge(pv_done, SLOTS * seq + 2 * g + 2)
                wait(act, o_turned, 2 * seq + g // 2)
                act.activation(oT[:, g, :], ps_o[:, 0:S], ACT.Copy).then_inc(o_copied, 1)

            def step(j, par):
                if at(j, -3):
                    load_weights(2)
                for s in range(SLOTS):
                    if s == 1 and has(j + 2):
                        act.wait_ge(v_ready, j + 3)
                        wait(act, v_ones_ready, j - 1)
                        if at(j, -2):
                            act.wait_ge(mask_ready, 2)
                        for t in range(TT):
                            op = act.activation(
                                v_all[:, bass.ds((j + 2) % 4, 1), t, :].rearrange("p a c -> p (a c)"),
                                ps_m2[:, BANK["v"], t * H:(t + 1) * H], ACT.Copy,
                                scale=mask_col[:, bass.ds((j + 2) * TT + t, 1)])
                        op.then_inc(v_copied, 1)
                    if has(j):
                        wait(act, pv_done, SLOTS * j + s - 1)
                        for c in (2 * s, 2 * s + 1):
                            act.wait_ge(scores_ready, CHUNKS * j + c + 1)
                            at_head = 2 * (c % 2)
                            act.activation(pT[:, s % 2, at_head:at_head + 2, :], ps_sc[:, c % 3, :, :],
                                           ACT.Exp, scale=SCALE).then_inc(exp_done, 1)
                    if s == 0 and has(j - 1):
                        copy_out(j - 1, 3)
                    if s in (2, 4, 6) and has(j):
                        copy_out(j, s // 2 - 1)
                    if s == 1 and has(j + 2):
                        act.wait_ge(even_rotated, j + 3)
                        wait(act, hi_written, 32 * (j + 2))
                        act.activation(parts[:, :, 0, 0, :], rcos[:, 0:2, :], ACT.Copy).then_inc(qk_hi, 1)
                    if s == 2 and has(j + 2) and not at(j, *DVE_SPLITS):
                        act.wait_ge(odd_rotated, j + 3)
                        wait(act, hi_written, 32 * (j + 2))
                        act.activation(parts[:, :, 0, 1, :], rcos[:, 2:4, :], ACT.Copy).then_inc(qk_hi, 1)
                    if s == 1 and has(j):
                        copy_max(j, 1)
                    if s == 3 and has(j + 3):
                        act.wait_ge(xn_turned, j + 4)
                        if at(j, -3):
                            act.wait_ge(aff_ready, 1)
                        wait(act, cos_done, 2 * (j + 3))
                        wait(act, sin_done, 2 * (j + 3))
                        for c in range(CC):
                            op = act.activation(h32[:, c, :], ps_m2[:, BANK["xn"], c * S:(c + 1) * S], ACT.Identity,
                                                scale=aff[:, 0, 0, c, bass.ds(j + 3, 1)],
                                                bias=aff[:, 0, 1, c, bass.ds(j + 3, 1)])
                        op.then_inc(h_copied, 1)
                    if s == 6 and at(j, -2, -1, 0):
                        load_weights(2 + j + 3)
                    if s == 4 and has(j - 1):
                        act.wait_ge(on_turned, j + 1)
                        wait(act, a_lo, j)
                        for c in range(CC):
                            op = act.activation(aT32[:, c, :], ps_m2[:, BANK["on"], c * S:(c + 1) * S], ACT.Identity,
                                                bias=vec("bv", c))
                        op.then_inc(a_copied, 1)
                    if s == 4 and has(j + 1):
                        copy_max(j + 1, 0)
                    if s in (5, 6) and has(j + 3):
                        e = s - 5
                        act.wait_ge(qk_ready, 2 * (j + 3) + e + 1)
                        if e == 0:
                            act.wait_ge(h_lo, j + 4)
                        for k in range(2):
                            op = act.activation(qk32[:, 2 * e + k, :],
                                                ps_m2[:, bank(j, ("qk_even", "qk_odd")[e]), k * S:(k + 1) * S],
                                                ACT.Identity, bias=vec("bqk", 2 * e + k))
                        op.then_inc(qk_copied, 1)
                    if s == 7 and at(j, -3, -2, -1, 0):
                        weights_hi(2 + j + 3)
                    if at(j, B) and s in GELU_AHEAD:
                        gelu(GELU_AHEAD[s])

            def copy_norm2(t):
                act.wait_ge(xn2_turned, t + 1)
                act.wait_ge(h2_lo, t)
                for c in range(CC):
                    for b in range(2):
                        op = act.activation(h2_32[:, c, b * S:(b + 1) * S],
                                            ps_t[:, c, b * S:(b + 1) * S], ACT.Identity,
                                            scale=aff[:, 1, 0, c, bass.ds(2 * t + b, 1)],
                                            bias=aff[:, 1, 1, c, bass.ds(2 * t + b, 1)])
                op.then_inc(h2_copied, 1)

            def gelu(n):
                f = n % FC
                act.wait_ge(f_ready, n + 1)
                wait(act, g_lo, n - 1)
                act.activation(g32[:, n % 2, :], ps_f[:, n % 3, :], ACT.Gelu,
                               bias=vec("ff_b1", f)).then_inc(g_done, 1)
                wait(act, ff2_done, n - AHEAD + 1)
                act.activation(gs[:, n % AHEAD, 0, :], ps_f[:, n % 3, :], ACT.Gelu,
                               bias=vec("ff_b1", f)).then_inc(g_hi, 1)

            steps(act, step)
            for n in range(len(GELU_AHEAD), NBLK * FC):
                gelu(n)
                if n % FC == 3 and n // FC + 1 < NBLK:
                    copy_norm2(n // FC + 1)

        @block.vector
        def _(dve):
            def norm_stats(seq_tile, n, step_sem, count, rstd_before):
                for t in range(n):
                    op = dve.bn_stats(stats[:, t, :], x_sb[:, bass.ds(seq_tile + t, 1), :].rearrange(
                        "p a c -> p (a c)"))
                op.then_inc(step_sem, 1)
                lead(dve)
                dve.wait_ge(step_sem, count + 1)
                for t in range(n):
                    op = dve.bn_aggr(mv[:, t, :], stats[:, t, :])
                op.then_inc(step_sem, 1)
                dve.wait_ge(step_sem, count + 2)
                wait(dve, rstd_ready, rstd_before)
                dve.tensor_scalar(var_eps[:, 0:n], mv[:, 0:n, 1:2].rearrange("p n a -> p (n a)"),
                                  EPS, None, ALU.add).then_inc(var_ready, 1)

            def norm_rows(rows, seq_tile, n, rstd_count, ready):
                dve.wait_ge(rstd_ready, rstd_count)
                for t in range(n):
                    op = dve.tensor_scalar(rows[:, t, :], x_sb[:, bass.ds(seq_tile + t, 1), :].rearrange(
                        "p a c -> p (a c)"), mv[:, t, 0:1], rstd[:, t:t + 1], ALU.subtract, ALU.mult)
                op.then_inc(ready, 1)

            def first_weights_lo(n):
                cols = slice(n * W_CHUNK, (n + 1) * W_CHUNK)
                first = (stage[:], rsin[:, :, :].rearrange("p a s -> p (a s)"))
                dve.wait_ge(w_first_hi, n + 1)
                dve.tensor_tensor(wts[:, 1, cols], first[n], wts[:, 0, cols].bitcast(F32),
                                  ALU.subtract).then_inc(w_first, 1)

            def adaptive(n):
                dve.wait_ge(mod_ready, n + 1)
                dve.wait_ge(vecs_in, 16)
                first_col = VECS[f"ada{n + 1}_b"][0]
                dve.tensor_tensor(
                    ada_mod[:, n, :, :],
                    ps_mod[n].rearrange("p (a b) -> p a b", b=B),
                    vecs[:, first_col:first_col + 2 * CC].unsqueeze(2).to_broadcast([P, 2 * CC, B]),
                    ALU.add).then_inc(mod_added, 1)
                dve.wait_ge(mod_added, n + 1)
                for c in range(CC):
                    dve.tensor_scalar(aff[:, n, 0, c, :], ada_mod[:, n, CC + c, :], 1.0,
                                      vec(f"ln{n + 1}_g", c), ALU.add, ALU.mult)
                    dve.tensor_scalar(aff[:, n, 1, c, :], ada_mod[:, n, CC + c, :], 1.0,
                                      vec(f"ln{n + 1}_b", c), ALU.add, ALU.mult).then_inc(aff_half, 1)
                dve.wait_ge(aff_half, CC * (n + 1))
                dve.tensor_tensor(aff[:, n, 1, :, :], aff[:, n, 1, :, :], ada_mod[:, n, 0:CC, :],
                                  ALU.add).then_inc(aff_ready, 1)

            def split_max(seq, half):
                dve.wait_ge(max_taken, NH * seq + HALF * (half + 1))
                wait(dve, max_turned, 2 * (seq - 1) + half + 1)
                dve.tensor_copy(mparts[:, half, :, 0, :].bitcast(F32R), m32[:, half, :, :]).then_inc(max_hi, 1)
                dve.wait_ge(max_hi, 2 * seq + half + 1)
                dve.tensor_tensor(mparts[:, half, :, 1, :], m32[:, half, :, :], mparts[:, half, :, 0, :],
                                  ALU.subtract).then_inc(max_lo, 1)

            def normalise(seq, pair):
                bank = ps_m2[:, BANK[f"o{pair}"], :]
                dve.wait_ge(o_turned, 2 * seq + pair + 2)
                dve.reciprocal(rden[:], bank.rearrange("p (n d) -> p n d", d=2 * HD)[:, :, HD:HD + 1]
                               .rearrange("p n a -> p (n a)")).then_inc(den_done, 1)
                dve.wait_ge(den_done, 2 * seq + pair + 1)
                wait(dve, on_turned, seq + 1)
                num = bank.rearrange("p (g t j d) -> p g t j d", g=2, t=TT, j=G4)
                den = rden[:].rearrange("p (g t j) -> p g t j", g=2, t=TT)
                for t in range(TT):
                    op = dve.tensor_tensor(
                        o_n[:, t, pair * P:(pair + 1) * P].rearrange("p (g j d) -> p g j d", g=2, j=G4),
                        num[:, :, t, :, 0:HD],
                        den[:, :, t, :].unsqueeze(3).to_broadcast([P, 2, G4, HD]), ALU.mult)
                op.then_inc(o_normed, 1)

            def take_max(seq, h):
                dve.wait_ge(max_scores, NH * seq + h + 1)
                if h % HALF == 0:
                    wait(dve, max_lo, 2 * (seq - 1) + h // HALF + 1)
                dve.tensor_reduce(
                    m32[:, h // HALF, :, h % HALF:h % HALF + 1].rearrange("p t a -> p (t a)"),
                    ps_max[:, h % 2, :].rearrange("p (t n) -> p t n", t=TT),
                    AX_X, ALU.max).then_inc(max_taken, 1)

            def split_gelu(n):
                dve.wait_ge(g_done, n + 1)
                dve.wait_ge(g_hi, n + 1)
                dve.tensor_tensor(gs[:, n % AHEAD, 1, :], g32[:, n % 2, :],
                                  gs[:, n % AHEAD, 0, :].bitcast(F32), ALU.subtract).then_inc(g_lo, 1)

            def step(j, par):
                for s in range(SLOTS):
                    if has(j + 1):
                        take_max(j + 1, 2 * s)
                        take_max(j + 1, 2 * s + 1)
                    if s == 0 and has(j + 3) and not at(j, -3, *LN_EARLY):
                        norm_stats((j + 3) * TT, TT, norm_step, 2 * (j + 3), j + 3)
                    if s == 4 and at(j, -3):
                        first_weights_lo(1)
                        dve.wait_ge(small_in, 16 * 4)
                        dve.tensor_copy(mask_col[:], mask_u8[:]).then_inc(mask_ready, 1)
                        dve.tensor_scalar(mask_row[:], mrow_u8[:], -1.0, MASKED,
                                          ALU.add, ALU.mult).then_inc(mask_ready, 1)
                    if s == 5 and at(j + 1, *LN_EARLY):
                        dve.wait_ge(x_in, 16 * (B - 1))
                        norm_stats((j + 4) * TT, TT, norm_step, 2 * (j + 4), j + 4)
                        dve.wait_ge(xn_turned, j + 4)
                        norm_rows(xn, (j + 4) * TT, TT, j + 5, xn_ready)
                    if s == 1 and has(j + 3) and not at(j, -3, *LN_EARLY):
                        wait(dve, xn_turned, j + 3)
                        norm_rows(xn, (j + 3) * TT, TT, j + 4, xn_ready)
                    if s == 1 and at(j, *DVE_SPLITS):
                        dve.wait_ge(odd_rotated, j + 3)
                        wait(dve, hi_written, 32 * (j + 2))
                        dve.tensor_copy(parts[:, :, 0, 1, :], rcos[:, 2:4, :]).then_inc(qk_hi, 1)
                        qk_lo_part(dve, j + 2)
                    if s == 2 and has(j - 1):
                        normalise(j - 1, 1)
                    if s == 0 and at(j, B - 1):
                        norm_stats(0, BT, n2_step, 0, B)
                    if s == 3 and at(j, B - 1):
                        dve.wait_ge(v_ones_ready, B)
                        norm_rows(xn2, 0, BT, B + 1, xn2_ready)
                    if s == (2 if at(j, -1) else 4) and has(j + 3):
                        dve.wait_ge(h_copied, j + 4)
                        wait(dve, v_ready, j + 3)
                        dve.tensor_copy(hs[:, 0, :, :], h32).then_inc(h_hi, 1)
                        dve.wait_ge(h_hi, j + 4)
                        dve.tensor_tensor(hs[:, 1, :, :], h32, hs[:, 0, :, :].bitcast(F32),
                                          ALU.subtract).then_inc(h_lo, 1)
                    if s == 3 and has(j + 1):
                        split_max(j + 1, 0)
                    if s == 7 and has(j - 1):
                        dve.wait_ge(attn_ready, j + 1)
                        dve.wait_ge(bo_added, j)
                        rows = x_sb[:, bass.ds((j - 1) * TT, TT), :]
                        dve.tensor_tensor(rows, ps_m2[:, BANK["proj_o"], :].rearrange("p (t c) -> p t c", t=TT), rows,
                                          ALU.add).then_inc(attn_added, 1)
                    if s == 5 and has(j - 1):
                        dve.wait_ge(a_copied, j)
                        wait(dve, attn_ready, j)
                        dve.tensor_copy(a_s[:, 0, :, :], aT32[:]).then_inc(a_hi, 1)
                    if s == 5 and at(j, B - 1):
                        dve.wait_ge(xn2_turned, 1)
                        dve.wait_ge(qk_lo, B)
                        for c in range(CC):
                            for b in range(2):
                                op = dve.tensor_scalar(h2_32[:, c, b * S:(b + 1) * S], ps_t[:, c, b * S:(b + 1) * S],
                                                       aff[:, 1, 0, c, b:b + 1], aff[:, 1, 1, c, b:b + 1],
                                                       ALU.mult, ALU.add)
                        op.then_inc(h2_copied, 1)
                    if s == 5 and has(j):
                        normalise(j, 0)
                    if s == 6 and at(j, B - 1):
                        dve.wait_ge(h2_copied, 1)
                        dve.wait_ge(scores_ready, CHUNKS * (B - 1))
                        dve.tensor_copy(h2s[:, 0, 0, :, :], h2_32).then_inc(h2_hi, 1)
                        dve.wait_ge(h2_hi, 1)
                        dve.tensor_tensor(h2s[:, 0, 1, :, :], h2_32, h2s[:, 0, 0, :, :].bitcast(F32),
                                          ALU.subtract).then_inc(h2_lo, 1)
                    if s in (6, 7) and has(j + 3):
                        e = s - 6
                        dve.wait_ge(qk_copied, 2 * (j + 3) + e + 1)
                        wait(dve, qk_lo, j + 3)
                        dve.tensor_tensor(rcos[:, 2 * e:2 * e + 2, :], qk32[:, 2 * e:2 * e + 2, :],
                                          rope[:, 0:1, :].to_broadcast([P, 2, S]), ALU.mult).then_inc(cos_done, 1)
                    if s == 7 and has(j + 1):
                        split_max(j + 1, 1)
                    if s == 7 and at(j, *DVE_ROTATES):
                        dve.wait_ge(sin_done, 2 * (j + 4))
                        dve.wait_ge(cos_done, 2 * (j + 4))
                        rotate_even(dve)
                    if s == 3 and at(j, -1):
                        adaptive(1)
                    if s == 7 and at(j, 0):
                        weights_lo(dve, 5)
                    if s == 3 and at(j, B):
                        dve.wait_ge(xn2_turned, 1)
                        norm_rows(xn2, BT, BT, B + 2, xn2_ready)
                    if at(j, B) and s in LO_AHEAD:
                        split_gelu(LO_AHEAD[s])
                    if s == 7 and at(j, B - 1):
                        norm_stats(BT, BT, n2_step, 2, B + 1)

            dve.wait_ge(x_first_in, 16)
            norm_stats(0, TT, norm_step, 0, 0)
            norm_rows(xn, 0, TT, 1, xn_ready)
            first_weights_lo(0)
            adaptive(0)
            steps(dve, step)

            def add_residual(t):
                for b in range(2):
                    if b == 0:
                        dve.wait_ge(y_ready, t + 1)
                    else:
                        dve.wait_ge(ff2_done, (t + 1) * FC)
                    dve.wait_ge(bff2_added, t + 1)
                    wait(dve, out_written[b], 16 * t)
                    dve.tensor_tensor(y_sb[:, b * TT:(b + 1) * TT, :], ps_y[:, b * TT:(b + 1) * TT, :],
                                      x_sb[:, t * BT + b * TT:t * BT + (b + 1) * TT, :],
                                      ALU.add).then_inc(y_added, 1)

            for n in range(len(LO_AHEAD), NBLK * FC):
                t, f = n // FC, n % FC
                split_gelu(n)
                if f == 2 and t > 0:
                    add_residual(t - 1)
                k = (n + 9) // FC
                if 2 <= k < NBLK and n == 8 * k - 9:
                    dve.wait_ge(attn_added, (k + 1) * BT // TT)
                    norm_stats(k * BT, BT, n2_step, 2 * k, B + k)
                if 2 <= k < NBLK and n == 8 * k - 8:
                    dve.wait_ge(xn2_turned, k)
                    norm_rows(xn2, k * BT, BT, B + k + 1, xn2_ready)
            add_residual(NBLK - 1)

        @block.tensor
        def _(pe):
            for free in (o_turned, on_turned, attn_ready):
                pe.sem_inc(free, 1)
            ada = pT[:, :, :, :].rearrange("p n g s -> p n (g s)").rearrange(
                "p n (c m) -> p n c m", c=CC)

            def modulate(n):
                pe.wait_ge(cond_in, 16)
                pe.wait_ge(ada_in[n], 16)
                for m in range(2 * CC):
                    for c in range(CC):
                        op = pe.matmul(ps_mod[n][:, m * B:(m + 1) * B],
                                       ada[:, n, c, m * P:(m + 1) * P], condT[:, c, :],
                                       start=(c == 0), stop=(c == CC - 1))
                op.then_inc(mod_ready, 1)

            modulate(0)
            pe.wait_ge(ident_in, 16)

            def w(l, col, n):
                return wts[:, l, col:col + n]

            def score_max(seq, par, h):
                if h % HALF == 0:
                    pe.wait_ge(stack_in[h // HALF], 80 * (seq + 1))
                wait(pe, max_taken, NH * seq + h - 1)
                for t in range(TT):
                    op = pe.matmul(ps_max[:, h % 2, t * S:(t + 1) * S],
                                   qs[0:ROWS_A, par, h, t * P:(t + 1) * P], ks[0:ROWS_A, par, h, :],
                                   start=True, stop=True)
                op.then_inc(max_scores, 1)

            def score_exp(seq, par, s):
                g, kt = s // 2, s % 2
                if s == 0 and at(seq, 0):
                    pe.wait_ge(mod_added, 2)
                if s % (SLOTS // 2) == 0:
                    pe.wait_ge(maxrow_in[s // (SLOTS // 2)], 32 * (seq + 1))
                for c in (2 * s, 2 * s + 1):
                    wait(pe, exp_done, CHUNKS * seq + (c - 2 if c >= 3 else {0: 0, 1: -2, 2: -1}[c]))
                    for i in range(2):
                        h = g * G4 + 2 * (c % 2) + i
                        op = pe.matmul(ps_sc[:, c % 3, i, :], ks[0:ROWS_B, par, h, kt * P:(kt + 1) * P],
                                       qs[0:ROWS_B, par, h, :], start=True, stop=True)
                    op.then_inc(scores_ready, 1)

            def times_v(seq, par, s):
                g, kt = s // 2, s % 2
                if s == 0:
                    pe.wait_ge(v_ones_ready, seq + 1)
                pe.wait_ge(exp_done, CHUNKS * seq + 2 * s + 2)
                if kt == 0:
                    wait(pe, o_copied, NH // G4 * seq + g)
                for i in range(G4):
                    op = pe.matmul(ps_o[i * 32:(i + 1) * 32, 0:S], v_ones[:, par, kt, g * G4 + i, :],
                                   pT[:, s % 2, i, :], start=(kt == 0), stop=(kt == TT - 1))
                op.then_inc(pv_done, 1)

            def turn_max(seq, half):
                pe.wait_ge(max_lo, 2 * seq + half + 1)
                for t in range(TT):
                    op = pe.transpose(ps_m2[0:2 * HALF, BANK[f"max{half}"], t * P:(t + 1) * P],
                                      mparts[:, half, t, :, :].rearrange("p l h -> p (l h)"), ident[:])
                op.then_inc(max_turned, 1)

            def turn_out(seq, pair):
                pe.wait_ge(o_copied, NH // G4 * seq + 2 * pair + 2)
                for g in range(2):
                    for t in range(TT):
                        col = (g * TT + t) * P
                        op = pe.transpose(ps_m2[:, BANK[f"o{pair}"], col:col + P],
                                          oT[:, 2 * pair + g, t * P:(t + 1) * P], ident[:])
                op.then_inc(o_turned, 1)

            def turn_rows(src, name, done):
                for c in range(CC):
                    for t in range(TT):
                        op = pe.transpose(ps_m2[:, BANK[name], c * S + t * P:c * S + (t + 1) * P],
                                          src[:, t, c * P:(c + 1) * P], ident[:])
                op.then_inc(done, 1)

            def rows_times(acts, col, name, done):
                for t in range(TT):
                    for n, (lw, la) in enumerate(PARTS):
                        for c in range(CC):
                            op = pe.matmul(ps_m2[:, BANK[name], t * H:(t + 1) * H], acts[:, la, c, t * P:(t + 1) * P],
                                           w(lw, col + c * H, H), start=(n == 0 and c == 0),
                                           stop=(n == 2 and c == CC - 1))
                op.then_inc(done, 1)

            def misc(j, name):
                if name == "max1":
                    turn_max(j, 1)
                if name == "max0":
                    turn_max(j + 1, 0)
                if name == "o1":
                    turn_out(j - 1, 1)
                if name == "o0":
                    turn_out(j, 0)
                if name == "on":
                    pe.wait_ge(o_normed, 2 * j)
                    turn_rows(o_n, name, on_turned)
                if name == "xn":
                    pe.wait_ge(xn_ready, j + 4)
                    turn_rows(xn, name, xn_turned)
                if name == "proj_o":
                    pe.wait_ge(a_lo, j + 1)
                    rows_times(a_s, W_O, name, attn_ready)
                if name == "v":
                    if at(j, -2):
                        pe.wait_ge(w_first, 2)
                    rows_times(hs, W_V, name, v_ready)
                if name in ("qk_even", "qk_odd"):
                    e = 0 if name == "qk_even" else 1
                    if e == 0:
                        pe.wait_ge(h_hi, j + 4)
                        if at(j, -3):
                            pe.wait_ge(w_first, 1)
                    for n, k in ((0, 0), (1, 0), (0, 1), (1, 1), (2, 0), (2, 1)):
                        lw, la = PARTS[n]
                        if e == 0 and (n, k) == (2, 0):
                            pe.wait_ge(h_lo, j + 4)
                        for c in range(CC):
                            op = pe.matmul(ps_m2[:, bank(j, name), k * S:(k + 1) * S],
                                           w(lw, W_QK + (c * 4 + 2 * e + k) * P, P), hs[:, la, c, :],
                                           start=(n == 0 and k == 0 and c == 0),
                                           stop=(n == 2 and c == CC - 1), skip_group_check=True)
                    op.then_inc(qk_ready, 1)
                    if e == 1 and at(j, -2):
                        modulate(1)

            def step(j, par):
                def turns(place, skip=()):
                    for index, (where, name, off, _, _, _) in enumerate(MISC):
                        if where == place and has(j + off) and name not in skip:
                            wait_bank(pe, j, index)
                            misc(j, name)

                for s in range(SLOTS):
                    if has(j):
                        score_exp(j, par, s)
                    turns(EARLY + s)
                    if s == 0 and at(j, -1):
                        turns(0)
                        turns(2, skip=("on",))
                    if s == 4 and at(j, B - 1):
                        turn_norm2(0)
                    if s == 6 and at(j, B):
                        turn_norm2(1)
                    if at(j, B) and s in FF1_AHEAD:
                        ff1(FF1_AHEAD[s])
                    if has(j + 1):
                        score_max(j + 1, 1 - par, 2 * s)
                        score_max(j + 1, 1 - par, 2 * s + 1)
                    if s == 0 and has(j - 1):
                        times_v(j - 1, 1 - par, SLOTS - 1)
                    if s > 0 and has(j):
                        times_v(j, par, s - 1)
                    if not (at(j, -1) and s in (0, 2)):
                        turns(s)

            def turn_norm2(t):
                pe.wait_ge(xn2_ready, t + 1)
                if t == 0:
                    pe.wait_ge(max_taken, NH * B)
                else:
                    pe.wait_ge(h2_copied, t)
                for c in range(CC):
                    for i in range(BT):
                        op = pe.transpose(ps_t[:, c, i * P:(i + 1) * P], xn2[:, i, c * P:(c + 1) * P], ident[:])
                op.then_inc(xn2_turned, 1)

            def ff1(n):
                t, f = n // FC, n % FC
                if f == 0:
                    pe.wait_ge(h2_lo, t + 1)
                if n == 0:
                    pe.wait_ge(w_split, 4)
                if n < 3:
                    pe.wait_ge(exp_done, CHUNKS * B)
                else:
                    pe.wait_ge(g_hi, n - 2)
                for k, (lw, la) in enumerate(PARTS):
                    for c in range(CC):
                        op = pe.matmul(ps_f[:, n % 3, :], w(lw, W_1 + c * FF + f * P, P), h2s[:, t, la, c, :],
                                       start=(k == 0 and c == 0), stop=(k == 2 and c == CC - 1))
                op.then_inc(f_ready, 1)

            def ff2(n):
                t, f = n // FC, n % FC
                pe.wait_ge(g_lo, n + 1)
                for i in range(BT):
                    if f == 0 and i % 2 == 0:
                        if t == 0:
                            pe.wait_ge(attn_added, B)
                        else:
                            pe.wait_ge(y_added, 2 * (t - 1) + i // 2 + 1)
                    for k, (lw, la) in enumerate(PARTS):
                        op = pe.matmul(ps_y[:, i, :], gs[:, n % AHEAD, la, i * P:(i + 1) * P],
                                       w(lw, W_2 + f * H, H), start=(f == 0 and k == 0 and i % 2 == 0),
                                       stop=(f == FC - 1 and k == 2), skip_group_check=True)
                    if f == FC - 1 and i == 1:
                        op.then_inc(y_ready, 1)
                op.then_inc(ff2_done, 1)

            steps(pe, step)
            for n in range(NBLK * FC):
                ff2(n)
                if n + AHEAD < NBLK * FC:
                    ff1(n + AHEAD)
                if n % FC == 6 and n // FC + 2 < NBLK:
                    turn_norm2(n // FC + 2)


def _chunks(a):
    c = a.shape[0] // P
    return a.reshape(c, P, -1).transpose(1, 0, 2).reshape(P, -1)


def kernel(**inputs):
    import numpy as np
    import concourse.bacc as bacc
    from concourse.bass_utils import run_bass_kernel_spmd

    a = {k.removeprefix("L0_cond_"): np.asarray(v) for k, v in inputs.items()}

    def rotary_columns(w, odd):
        return w.reshape(w.shape[0], NH, ROT, 2)[:, :, :, odd].transpose(0, 2, 1).reshape(w.shape[0], P)

    qk = np.concatenate([rotary_columns(a[n], odd) for odd in (0, 1) for n in ("wq", "wk")], axis=1)
    weights = np.concatenate([_chunks(w) for w in (qk, a["wv"], a["wo"], a["ff_w1"], a["ff_w2"])], axis=1)
    bqk = np.concatenate([rotary_columns(a[n][None], odd) for odd in (0, 1) for n in ("bq", "bk")], axis=0)
    vecs = np.concatenate([bqk.T] + [a[n].reshape(-1, P).T for n in (
        "bv", "ln1_g", "ln1_b", "ada1_b", "ln2_g", "ln2_b", "ada2_b", "ff_b1")], axis=1)
    inv = (np.float32(1.0) / np.power(np.float32(10000.0), np.arange(ROT, dtype=np.float32) / np.float32(ROT)))
    ang = np.arange(S, dtype=np.float32)[:, None] * inv.astype(np.float32)[None, :]
    rope = np.stack([np.cos(ang), np.sin(ang)]).transpose(2, 0, 1).astype(np.float32)
    arrays = {
        "x": a["x"],
        "condT": a["cond_1024"].reshape(B, CC, P).transpose(2, 1, 0),
        "mask_row": a["mask_BxS_bf1"].view(np.uint8),
        "mask_col": a["mask_BxS_bf1"].view(np.uint8).reshape(B * TT, P).T,
        "weights": weights,
        "ada": np.concatenate([_chunks(a["ada1_w"]), _chunks(a["ada2_w"])], axis=1),
        "vecs": vecs,
        "rope": np.repeat(rope, NH, axis=0),
        "bo": a["bo"],
        "bff2": a["ff_b2"],
        "ident": np.eye(P, dtype=np.float32),
    }
    arrays = {f"{k}_dram": np.ascontiguousarray(v) for k, v in arrays.items()}
    nc = bacc.Bacc("TRN2", target_bir_lowering=False, num_devices=1)
    args = [nc.dram_tensor(k, v.shape, mybir.dt.from_np(v.dtype), kind="ExternalInput").ap()
            for k, v in arrays.items()]
    out = nc.dram_tensor("out_dram", (B, S, H), F32, kind="ExternalOutput").ap()
    block_kernel(nc, *args, out)
    r = run_bass_kernel_spmd(nc, [arrays], core_ids=[0])
    return r.results[0]["out_dram"]
```
